# Optimizing a Trainium2 kernel written in Bass

```python
import numpy as np
import jax
import jax.numpy as jnp

def _softmax(x, axis=-1):
    return jax.nn.softmax(x, axis=axis)

def _gelu(x):
    return jax.nn.gelu(x, approximate=True)

def _silu(x):
    return jax.nn.silu(x)

def _sigmoid(x):
    return jax.nn.sigmoid(x)

def _layernorm(x, axis=-1, eps=1e-05):
    m = jnp.mean(x, axis=axis, keepdims=True)
    v = jnp.var(x, axis=axis, keepdims=True)
    return (x - m) / jnp.sqrt(v + eps)

def _scatter_add(tgt, idx, src, axis=0):
    return tgt.at[idx].add(src)

def _segment_sum(src, seg, n):
    return jax.ops.segment_sum(src, seg, n)
kernel_name = 'mk_cond_seq_d1_seqx_r8_391b67'

def setup_inputs(seed: int=0):
    np.random.seed(seed)
    _w = jnp.asarray

    def _rec_inputs():
        import jax
        import jax.numpy as jnp
        _rk = jax.random.key(seed)
        x = 7.22e-05 + 1 * jax.random.normal(jax.random.fold_in(_rk, 1), (128, 32, 128), jnp.float32)
        _lenS = 32 - jax.random.randint(jax.random.fold_in(_rk, 7), (128,), 0, max(1, 32 // 4) + 1, jnp.int32)
        _lenS2 = 32 - jax.random.randint(jax.random.fold_in(_rk, 8), (128,), 0, max(1, 32 // 4) + 1, jnp.int32)
        cond_1024 = 0.0061147 + 1.02565 * jax.random.normal(jax.random.fold_in(_rk, 11), (128, 128), jnp.float32)
        return (x, cond_1024)
    x, cond_1024 = _rec_inputs()

    def _L0_cond_setup():
        import jax, jax.numpy as jnp
        import numpy as np
        D_MODEL = 128
        NHEAD = 16
        HEAD_DIM = D_MODEL // NHEAD
        D_FF = 512
        EPS = 1e-05

        def _layernorm(x):
            mu = jnp.mean(x, axis=-1, keepdims=True)
            var = jnp.var(x, axis=-1, keepdims=True)
            return (x - mu) * jax.lax.rsqrt(var + EPS)
        key = jax.random.key(seed)
        ks = jax.random.split(key, 16)
        B, N = (4, 256)
        s = 0.02
        inp = {'x': jax.random.normal(ks[0], (B, N, D_MODEL), jnp.float32), 'c': jax.random.normal(ks[1], (B, D_MODEL), jnp.float32), 'W_ada': jax.random.normal(ks[2], (D_MODEL, 6 * D_MODEL), jnp.float32) * s, 'b_ada': jnp.zeros((6 * D_MODEL,), jnp.float32), 'Wq': jax.random.normal(ks[3], (D_MODEL, D_MODEL), jnp.float32) * s, 'bq': jnp.zeros((D_MODEL,), jnp.float32), 'Wk': jax.random.normal(ks[4], (D_MODEL, D_MODEL), jnp.float32) * s, 'bk': jnp.zeros((D_MODEL,), jnp.float32), 'Wv': jax.random.normal(ks[5], (D_MODEL, D_MODEL), jnp.float32) * s, 'bv': jnp.zeros((D_MODEL,), jnp.float32), 'Wo': jax.random.normal(ks[6], (D_MODEL, D_MODEL), jnp.float32) * s, 'bo': jnp.zeros((D_MODEL,), jnp.float32), 'W1': jax.random.normal(ks[7], (D_MODEL, D_FF), jnp.float32) * s, 'b1': jnp.zeros((D_FF,), jnp.float32), 'W2': jax.random.normal(ks[8], (D_FF, D_MODEL), jnp.float32) * s, 'b2': jnp.zeros((D_MODEL,), jnp.float32)}
        return inp
    _L0_cond_all = _L0_cond_setup()
    _L0_cond_in = {k: v for k, v in _L0_cond_all.items() if k in ('W_ada', 'b_ada', 'Wq', 'bq', 'Wk', 'bk', 'Wv', 'bv', 'Wo', 'bo', 'W1', 'b1', 'W2', 'b2')}
    del _L0_cond_all
    return {'x': x, 'cond_1024': cond_1024, 'L0_cond_W_ada': _L0_cond_in['W_ada'], 'L0_cond_b_ada': _L0_cond_in['b_ada'], 'L0_cond_Wq': _L0_cond_in['Wq'], 'L0_cond_bq': _L0_cond_in['bq'], 'L0_cond_Wk': _L0_cond_in['Wk'], 'L0_cond_bk': _L0_cond_in['bk'], 'L0_cond_Wv': _L0_cond_in['Wv'], 'L0_cond_bv': _L0_cond_in['bv'], 'L0_cond_Wo': _L0_cond_in['Wo'], 'L0_cond_bo': _L0_cond_in['bo'], 'L0_cond_W1': _L0_cond_in['W1'], 'L0_cond_b1': _L0_cond_in['b1'], 'L0_cond_W2': _L0_cond_in['W2'], 'L0_cond_b2': _L0_cond_in['b2']}

def reference(x, cond_1024, L0_cond_W_ada, L0_cond_b_ada, L0_cond_Wq, L0_cond_bq, L0_cond_Wk, L0_cond_bk, L0_cond_Wv, L0_cond_bv, L0_cond_Wo, L0_cond_bo, L0_cond_W1, L0_cond_b1, L0_cond_W2, L0_cond_b2):
    import jax
    import jax.numpy as jnp

    def _L0_cond_ref(x, c, W_ada, b_ada, Wq, bq, Wk, bk, Wv, bv, Wo, bo, W1, b1, W2, b2):
        import jax, jax.numpy as jnp
        import numpy as np
        D_MODEL = 128
        NHEAD = 16
        HEAD_DIM = D_MODEL // NHEAD
        D_FF = 512
        EPS = 1e-05

        def _layernorm(x):
            mu = jnp.mean(x, axis=-1, keepdims=True)
            var = jnp.var(x, axis=-1, keepdims=True)
            return (x - mu) * jax.lax.rsqrt(var + EPS)
        B, N, _ = x.shape
        ada = (c @ W_ada + b_ada)[:, None, :]
        shift1, scale1, gate1, shift2, scale2, gate2 = jnp.split(ada, 6, axis=-1)
        h = _layernorm(x) * (1.0 + scale1) + shift1
        Q = (h @ Wq + bq).reshape(B, N, NHEAD, HEAD_DIM)
        K = (h @ Wk + bk).reshape(B, N, NHEAD, HEAD_DIM)
        V = (h @ Wv + bv).reshape(B, N, NHEAD, HEAD_DIM)
        scores = jnp.einsum('bqhd,bkhd->bhqk', Q, K) / np.sqrt(HEAD_DIM).astype(np.float32)
        attn = jax.nn.softmax(scores, axis=-1)
        attn_out = jnp.einsum('bhqk,bkhd->bqhd', attn, V).reshape(B, N, D_MODEL)
        attn_out = attn_out @ Wo + bo
        x = x + gate1 * attn_out
        h = _layernorm(x) * (1.0 + scale2) + shift2
        ff = jax.nn.gelu(h @ W1 + b1, approximate=False) @ W2 + b2
        return x + gate2 * ff
    x = _L0_cond_ref(x, cond_1024, L0_cond_W_ada, L0_cond_b_ada, L0_cond_Wq, L0_cond_bq, L0_cond_Wk, L0_cond_bk, L0_cond_Wv, L0_cond_bv, L0_cond_Wo, L0_cond_bo, L0_cond_W1, L0_cond_b1, L0_cond_W2, L0_cond_b2)
    return x

_drawn_inputs = setup_inputs


def setup_inputs(seed=0):
    import zlib

    import numpy as np

    out = dict(_drawn_inputs(seed))
    spreads = {'L0_cond_b_ada': (0.0, 0.563),
     'L0_cond_bq': (0.0, 0.8),
     'L0_cond_bk': (0.0, 0.8),
     'L0_cond_bv': (0.0, 0.8),
     'L0_cond_bo': (0.0, 0.323),
     'L0_cond_b1': (0.0, 0.8),
     'L0_cond_b2': (0.0, 0.316)}
    factors = {'L0_cond_Wq': 8.0,
     'L0_cond_Wk': 8.0,
     'L0_cond_Wv': 8.0,
     'L0_cond_Wo': 7.864,
     'L0_cond_W1': 3.954,
     'L0_cond_W2': 3.566}
    for name, (base, spread) in spreads.items():
        noise = np.random.default_rng([zlib.crc32(name.encode()), seed]).standard_normal(out[name].shape)
        drawn = base * np.exp(spread * noise) if base else spread * noise
        out[name] = jnp.asarray(drawn.astype(out[name].dtype))
    for name, factor in factors.items():
        out[name] = (out[name] * factor).astype(out[name].dtype)
    return out
```

```python
from contextlib import ExitStack

import concourse.bass as bass
from concourse import mybir

F32 = mybir.dt.float32
ALU = mybir.AluOpType
ACT = mybir.ActivationFunctionType
AX = mybir.AxisListType


class Step:

    def __init__(self, pair, parity):
        self.pair, self.parity = pair, parity
        self.t = pair * 2 + parity

    def plus(self, d):
        parity = (self.parity + d) % 2
        return Step(self.pair + (self.parity + d - parity) // 2, parity)


def dit_block(nc, x, cond, W_ada, b_ada, Wq, bq, Wk, bk, Wv, bv, Wo, bo, W1, b1, W2, b2, out):
    B, N, D = x.shape
    P = 128
    HD = 8
    H = D // HD
    Q4 = 4
    HQ = H // Q4
    FF = W1.shape[1]
    FC = FF // P
    GROUPS = B // Q4
    SB = 4
    T = SB * P
    NS = GROUPS // SB
    BS = SB * Q4
    VW = HD + 1
    EPS = 1e-05
    SCALE = float(1.0 / (HD ** 0.5))
    KINC = 16 * H
    FREE = 1
    assert N == 32 and D == P and B % (Q4 * SB) == 0 and NS % 2 == 0

    with ExitStack() as ctx:
        def sb(name, shape):
            return ctx.enter_context(nc.sbuf_tensor(name, shape, F32))

        def pb(name):
            return ctx.enter_context(nc.psum_tensor(name, [P, T], F32))

        def sem(name):
            return ctx.enter_context(nc.semaphore(name))

        x_sb = sb("x_sb", [P, NS * T])
        wada_sb = sb("wada_sb", [P, 6 * D])
        cond_sb = sb("cond_sb", [B, D])
        condT = sb("condT", [D, B])
        wq_sb, wk_sb, wv_in, wv_sb, wo_sb = (sb(n, [P, D]) for n in ("wq_sb", "wk_sb", "wv_in", "wv_sb", "wo_sb"))
        w1_sb = sb("w1_sb", [P, FF])
        w2_sb = sb("w2_sb", [P, FC * D])
        bias_rows = sb("bias_rows", [P, P])
        biasT = sb("biasT", [P, 15])
        ADA_B, Q_B, K_B, O_B, F2_B, F1_B, V_B = 0, 6, 7, 8, 9, 10, 14
        adaT = sb("adaT", [D, 6, B])
        ident = sb("ident", [P, P])
        minus_half = sb("minus_half", [P, GROUPS])
        bn = sb("bn", [P, GROUPS, 6])
        mean = [sb(f"mean{i}", [P, GROUPS]) for i in (1, 2)]
        rstd = [sb(f"rstd{i}", [P, GROUPS]) for i in (1, 2)]
        ln_dif, ln_m2, ln_sq, ln_var = (sb(n, [P, GROUPS]) for n in ("ln_dif", "ln_m2", "ln_sq", "ln_var"))
        xn = [sb(f"xn{i}", [P, T]) for i in range(2)]
        hT = [sb(f"hT{i}", [D, T]) for i in range(2)]
        qT = [sb(f"qT{i}", [P, T]) for i in range(2)]
        kT = [sb(f"kT{i}", [P, T]) for i in range(2)]
        vT = sb("vT", [P, T])
        vx = sb("vx", [P, T])
        kexp = [sb(f"kexp{i}", [P, H, T]) for i in range(2)]
        vexp = [sb(f"vexp{i}", [P, BS, Q4, HQ, VW]) for i in range(2)]
        smax = [sb(f"smax{i}", [P, H]) for i in range(2)]
        sdif = [sb(f"sdif{i}", [P, H * N]) for i in range(2)]
        prob = [sb(f"prob{i}", [P, H * N]) for i in range(2)]
        probT = [sb(f"probT{i}", [P, H * N]) for i in range(2)]
        rsum = [sb(f"rsum{i}", [P, H]) for i in range(2)]
        attn = [sb(f"attn{i}", [P, SB, D]) for i in range(2)]
        attnT = sb("attnT", [P, T])
        zT = sb("zT", [D, T])
        hid = sb("hid", [P, FC, T])

        ps_s = [pb("ps_s0"), pb("ps_s1")]
        ps_p = [pb("ps_p0"), pb("ps_p1")]
        ps_o = [pb("ps_o0"), pb("ps_o1")]
        ps_m = [pb("ps_m0"), pb("ps_m1")]
        ps_ff = [ps_s[0], ps_s[1], ps_m[1], ps_o[1]]

        x_in = [sem(f"x_in{t}") for t in range(NS)]
        (w_ada_in, w_qkv_in, w_late_in, rows_in) = map(sem, ("w_ada_in", "w_qkv_in", "w_late_in", "rows_in"))
        (rows_zero, id_zero, id_ready, consts_ready, kexp_zero, vexp_zero, vexp_ones, wv_ready) = map(sem, (
            "rows_zero", "id_zero", "id_ready", "consts_ready", "kexp_zero", "vexp_zero", "vexp_ones", "wv_ready"))
        (setupT_ready, setupT_copied, ada_ps, ada_ready) = map(sem, (
            "setupT_ready", "setupT_copied", "ada_ps", "ada_ready"))
        (bn_done, ln_step, ln_ready, rstd_ready, xn_sub, xn_ready) = map(sem, (
            "bn_done", "ln_step", "ln_ready", "rstd_ready", "xn_sub", "xn_ready"))
        (xnT_ps, h_scaled, h_ready) = map(sem, ("xnT_ps", "h_scaled", "h_ready"))
        (q_ps, k_ps, v_ps, q_ready, k_ready, v_ready, vx_ready, vexp_ready) = map(sem, (
            "q_ps", "k_ps", "v_ps", "q_ready", "k_ready", "v_ready", "vx_ready", "vexp_ready"))
        kexp_in = [sem(f"kexp_in{i}") for i in range(2)]
        (s_ps, max_ready, dif_ready, prob_ready, probT_ps, probT_ready, o_ps, rsum_ready, attn_ready) = map(sem, (
            "s_ps", "max_ready", "dif_ready", "prob_ready", "probT_ps", "probT_ready", "o_ps", "rsum_ready",
            "attn_ready"))
        (attnT_ps, attnT_ready, wo_ps, z_ready, zT_ps, x2_ready) = map(sem, (
            "attnT_ps", "attnT_ready", "wo_ps", "z_ready", "zT_ps", "x2_ready"))
        (ff_ps, hid_ready, w2_ps, z2_ready, z2T_ps, y_ready, y_out) = map(sem, (
            "ff_ps", "hid_ready", "w2_ps", "z2_ready", "z2T_ps", "y_ready", "y_out"))

        def tokens(t):
            return x_sb[:, bass.ds(t * T, T)]

        def ada(r, t):
            return adaT[:, r, bass.ds(t * BS, BS)].unsqueeze(2).to_broadcast([D, BS, N])

        def per_batch(ap):
            return ap.rearrange("p (b q) -> p b q", q=N)

        def per_group(stat, t):
            return stat[:, bass.ds(t * SB, SB)].unsqueeze(2).to_broadcast([P, SB, D])

        SHIFT1, SCALE1, GATE1, SHIFT2, SCALE2, GATE2 = range(6)
        block = ctx.enter_context(nc.Block())

        def both_phases_loop(eng, body):
            body(Step(0, 0), True, False)
            with eng.Fori(0, (NS - 2) // 2) as i:
                body(Step(i, 1), False, False)
                body(Step(i + 1, 0), False, False)
            body(Step(NS // 2 - 1, 1), False, True)

        @block.sync
        def _(sp):
            for t in range(NS):
                sp.dma_start(x_sb[:, t * T:(t + 1) * T].rearrange("p (g d) -> p g d", g=SB),
                             x[t * BS:(t + 1) * BS].rearrange("(g b) q d -> (b q) g d", g=SB)).then_inc(x_in[t], 16)
                if t == 0:
                    sp.wait_ge(rows_zero, 1)
                    rows = [(b_ada, ADA_B, 6), (bq, Q_B, 1), (bk, K_B, 1), (bo, O_B, 1), (b2, F2_B, 1), (b1, F1_B, FC)]
                    for src, r, n in rows:
                        sp.dma_start(bias_rows[r:r + n, :], src.rearrange("(r p) -> r p", p=P)).then_inc(rows_in, 16)
                    sp.dma_start(bias_rows[V_B:V_B + 1, :].rearrange("o (h g d) -> o h g d", h=Q4, g=HQ),
                                 bv.rearrange("(o g h d) -> o h g d", o=1, g=HQ, h=Q4)).then_inc(rows_in, 16)

            def expand_k(s):
                sp.wait_ge(k_ready, s.t + 1)
                sp.wait_ge(s_ps, s.t * SB - SB)
                for h in range(H):
                    rows = slice(h * HD, (h + 1) * HD)
                    sp.dma_start(kexp[s.parity][rows, h, :], kT[s.parity][rows, :]).then_inc(kexp_in[s.parity], 16)

            for t in range(2):
                sp.wait_ge(kexp_zero, t + 2)
                sp.wait_ge(k_ready, t + 1)
                for h in range(H):
                    rows = slice(h * HD, (h + 1) * HD)
                    sp.dma_start(kexp[t][rows, h, :], kT[t][rows, :]).then_inc(kexp_in[t], 16)
            with sp.Fori(1, NS // 2) as i:
                expand_k(Step(i, 0))
                expand_k(Step(i, 1))
            with sp.Fori(0, NS) as t:
                sp.wait_ge(y_ready, t + 1 + FREE)
                sp.dma_start(out[bass.ds(t * BS, BS)].rearrange("(g b) q d -> (b q) g d", g=SB),
                             tokens(t).rearrange("p (g d) -> p g d", g=SB)).then_inc(y_out, 16)
            sp.wait_ge(y_out, 16 * NS)

        @block.gpsimd
        def _(pool):
            pool.memset(bias_rows[:, :], 0.0).then_inc(rows_zero, 1)
            pool.memset(ident[:, :], 0.0).then_inc(id_zero, 1)
            pool.memset(minus_half[:, :], -0.5).then_inc(consts_ready, 1)
            pool.wait_ge(id_zero, 1)
            pool.affine_select(out=ident[:, :], in_=ident[:, :], compare_op=ALU.not_equal, fill=1.0, base=0,
                               pattern=[[-1, P]], channel_multiplier=1).then_inc(id_ready, 1)
            pool.wait_ge(w_qkv_in, 48)
            pool.tensor_copy(wv_sb[:, :].rearrange("p (h g d) -> p h g d", h=Q4, g=HQ),
                             wv_in[:, :].rearrange("p (g h d) -> p h g d", h=Q4, g=HQ)).then_inc(wv_ready, 1)
            pool.memset(kexp[0][:, H // 2:H, :], 0.0).then_inc(kexp_zero, 1)

            def rstd_of(ln, c0, c1, count):
                pool.wait_ge(ln_ready, count)
                pool.tensor_tensor(rstd[ln][:, c0:c1], ln_var[:, c0:c1], minus_half[:, c0:c1],
                                   ALU.pow).then_inc(rstd_ready, 1)

            def normalize(s, ln):
                n = ln * NS
                pool.wait_ge(xnT_ps, s.t - 1 + n)
                pool.wait_ge(consts_ready, 1)
                x3 = tokens(s.t).rearrange("p (g d) -> p g d", g=SB)
                xn3 = xn[s.parity][:, :].rearrange("p (g d) -> p g d", g=SB)
                nc.gpsimd.tensor_tensor(xn3, x3, per_group(mean[ln], s.t), ALU.subtract).then_inc(xn_sub, 1)
                pool.wait_ge(xn_sub, s.t + 1 + n)
                pool.wait_ge(consts_ready, 1)
                nc.gpsimd.tensor_tensor(xn3, xn3, per_group(rstd[ln], s.t), ALU.mult).then_inc(xn_ready, 1)

            def shift(s, ln):
                n = ln * NS
                pool.wait_ge(h_scaled, s.t + 1 + n)
                pool.wait_ge(consts_ready, 1)
                h = per_batch(hT[s.parity][:, :])
                nc.gpsimd.tensor_tensor(h, h, ada(SHIFT2 if ln else SHIFT1, s.t), ALU.add).then_inc(h_ready, 1)

            pool.wait_ge(consts_ready, 1)
            rstd_of(0, 0, SB, 1)
            pool.wait_ge(rstd_ready, 1)
            x3 = tokens(0).rearrange("p (g d) -> p g d", g=SB)
            xn3 = xn[0][:, :].rearrange("p (g d) -> p g d", g=SB)
            nc.gpsimd.tensor_tensor(xn3, x3, per_group(mean[0], 0), ALU.subtract).then_inc(xn_sub, 1)
            pool.wait_ge(xn_sub, 1)
            nc.gpsimd.tensor_tensor(xn3, xn3, per_group(rstd[0], 0), ALU.mult).then_inc(xn_ready, 1)
            shift(Step(0, 0), 0)
            rstd_of(0, SB, GROUPS, 2)
            for p in range(2):
                pool.memset(vexp[p][:, :, :, :, :], 0.0).then_inc(vexp_zero, 1)
            pool.wait_ge(vexp_zero, 2)
            for p in range(2):
                for h4 in range(Q4):
                    pool.memset(vexp[p][32 * h4:32 * h4 + 32, :, h4, :, HD:VW], 1.0).then_inc(vexp_ones, 1)
            pool.wait_ge(vexp_ones, 2 * Q4)
            pool.wait_ge(rstd_ready, 2)
            x3 = tokens(1).rearrange("p (g d) -> p g d", g=SB)
            xn3 = xn[1][:, :].rearrange("p (g d) -> p g d", g=SB)
            nc.gpsimd.tensor_tensor(xn3, x3, per_group(mean[0], 1), ALU.subtract).then_inc(xn_sub, 1)
            pool.wait_ge(xn_sub, 2)
            nc.gpsimd.tensor_tensor(xn3, xn3, per_group(rstd[0], 1), ALU.mult).then_inc(xn_ready, 1)
            pool.memset(kexp[1][:, :, :], 0.0).then_inc(kexp_zero, 1)
            normalize(Step(1, 0), 0)
            with pool.Fori(0, (NS - 4) // 2 + 0) as i:
                for d in (1, 2):
                    s = Step(i, 0).plus(d)
                    shift(s, 0)
                    normalize(s.plus(2), 0)
            shift(Step(NS // 2 - 2, 1), 0)
            normalize(Step(NS // 2 - 1, 1), 0)
            shift(Step(NS // 2 - 1, 0), 0)
            shift(Step(NS // 2 - 1, 1), 0)
            rstd_of(1, 0, (NS - 2) * SB, 3)
            pool.wait_ge(rstd_ready, 3)
            normalize(Step(0, 0), 1)
            normalize(Step(0, 1), 1)
            shift(Step(0, 0), 1)
            rstd_of(1, (NS - 2) * SB, GROUPS, 4)
            pool.wait_ge(rstd_ready, 4)
            normalize(Step(1, 0), 1)
            with pool.Fori(0, (NS - 4) // 2) as i:
                for d in (1, 2):
                    s = Step(i, 0).plus(d)
                    shift(s, 1)
                    normalize(s.plus(2), 1)
            shift(Step(NS // 2 - 2, 1), 1)
            normalize(Step(NS // 2 - 1, 1), 1)
            shift(Step(NS // 2 - 1, 0), 1)
            shift(Step(NS // 2 - 1, 1), 1)

        @block.tensor
        def _(pe):
            for done in (attnT_ps, wo_ps, zT_ps, w2_ps, z2T_ps):
                pe.sem_inc(done, FREE)

            def xn_transposes(s, ln):
                pe.wait_ge(xn_ready, s.t + 1 + ln * NS)
                bank = ps_p[s.parity] if ln else ps_m[0]
                for j in range(SB):
                    last = nc.tensor.transpose(bank[:, j * P:(j + 1) * P], xn[s.parity][:, j * P:(j + 1) * P],
                                               ident[:, :])
                last.then_inc(xnT_ps, 1)

            def project(s, w, bank, done):
                nc.tensor.matmul(bank[:, :], w[:, :], hT[s.parity][:, :], start=True, stop=True).then_inc(done, 1)

            def scores(s, j):
                for b in range(Q4):
                    q = slice(j * P + b * N, j * P + (b + 1) * N)
                    last = nc.tensor.matmul(ps_s[j % 2][b * N:(b + 1) * N, :], qT[s.parity][:, q],
                                            kexp[s.parity][:, :, q], start=True, stop=True)
                last.then_inc(s_ps, 1)

            def prob_transposes(j):
                for g in range(HQ):
                    c = slice(g * P, (g + 1) * P)
                    last = nc.tensor.transpose(ps_p[j % 2][:, c], prob[j % 2][:, c], ident[:, :])
                last.then_inc(probT_ps, 1)

            def values(s, j):
                for b in range(Q4):
                    for g in range(HQ):
                        o = g * Q4 * VW
                        last = nc.tensor.matmul(ps_o[j % 2][b * N:(b + 1) * N, o:o + Q4 * VW],
                                                probT[j % 2][:, g * P + b * N:g * P + (b + 1) * N],
                                                vexp[s.parity][:, j * Q4 + b, :, g, :], start=True, stop=True)
                last.then_inc(o_ps, 1)

            pe.wait_ge(id_ready, 1)
            pe.wait_ge(rows_in, 16 * 7)
            nc.tensor.transpose(ps_m[0][:, 0:P], bias_rows[:, :], ident[:, :]).then_inc(setupT_ready, 1)
            pe.wait_ge(w_ada_in, 32)
            nc.tensor.transpose(ps_m[1][:, 0:P], cond_sb[:, :], ident[:, :]).then_inc(setupT_ready, 1)
            pe.wait_ge(setupT_copied, 2)
            for r in range(6):
                bank, c = ps_o[r // 4], r % 4 * B
                nc.tensor.matmul(bank[:, c:c + B], wada_sb[:, r * D:(r + 1) * D], condT[:, :],
                                 start=True, stop=True).then_inc(ada_ps, 1)

            xn_transposes(Step(0, 0), 0)
            pe.wait_ge(h_ready, 1)
            pe.wait_ge(w_qkv_in, 48)
            project(Step(0, 0), wk_sb, ps_m[1], k_ps)
            project(Step(0, 0), wq_sb, ps_m[0], q_ps)
            pe.wait_ge(wv_ready, 1)
            pe.wait_ge(q_ready, 1)
            project(Step(0, 0), wv_sb, ps_m[0], v_ps)
            pe.wait_ge(kexp_in[0], KINC)
            scores(Step(0, 0), 0)

            def attend(s, first, final):
                for j in range(SB):
                    n = s.t * SB + j
                    if j < SB - 1:
                        if not (first and j == 0):
                            pe.wait_ge(dif_ready, n)
                        scores(s, j + 1)
                    elif not final:
                        nx = s.plus(1)
                        pe.wait_ge(dif_ready, n)
                        pe.wait_ge(q_ready, nx.t + 1)
                        pe.wait_ge(kexp_in[nx.parity], (nx.pair + 1) * KINC)
                        scores(nx, 0)
                    if j == 0 and not final:
                        if first:
                            pe.wait_ge(v_ready, 1)
                        else:
                            pe.wait_ge(x2_ready, s.t - 1 + FREE)
                        xn_transposes(s.plus(1), 0)
                    if j == 1 and not final:
                        pe.wait_ge(h_scaled, s.t + 2)
                        project(s.plus(1), wq_sb, ps_m[0], q_ps)
                    if j == 2 and not final:
                        pe.wait_ge(q_ready, s.t + 2)
                        project(s.plus(1), wv_sb, ps_m[0], v_ps)
                    if j == 3 and not first:
                        out_project(s.plus(-1))
                    pe.wait_ge(prob_ready, n + 1)
                    if not (first and j < 2):
                        pe.wait_ge(probT_ready, n - 1)
                    prob_transposes(j)
                    if not (first and j == 0):
                        before = s if j else s.plus(-1)
                        pe.wait_ge(probT_ready, n)
                        pe.wait_ge(vexp_ready, before.t * Q4 + Q4)
                        if not (first and j < 3):
                            pe.wait_ge(attn_ready, n - 2)
                        values(before, (j - 1) % SB)
                    if j == 0 and not final:
                        pe.wait_ge(h_ready, s.t + 2)
                        if first:
                            pe.wait_ge(k_ready, 1)
                        else:
                            pe.wait_ge(z_ready, s.t - 1 + FREE)
                        project(s.plus(1), wk_sb, ps_m[1], k_ps)
                    if j == 1 and not first:
                        attn_transposes(s.plus(-1), NS if final else s.t + 2)
                    if j == 3 and not first:
                        branch_transposes(s.plus(-1), NS if final else s.t + 2)

            def attn_transposes(s, k_read):
                pe.wait_ge(attn_ready, s.t * SB + SB)
                pe.wait_ge(k_ready, k_read)
                for j in range(SB):
                    last = nc.tensor.transpose(ps_m[1][:, j * P:(j + 1) * P], attn[s.parity][:, j, :], ident[:, :])
                last.then_inc(attnT_ps, 1)

            def out_project(s):
                pe.wait_ge(attnT_ready, s.t + 1)
                nc.tensor.matmul(ps_m[1][:, :], wo_sb[:, :], attnT[:, :], start=True, stop=True).then_inc(wo_ps, 1)

            def branch_transposes(s, v_read):
                pe.wait_ge(v_ready, v_read)
                pe.wait_ge(z_ready, s.t + 1 + FREE)
                for j in range(SB):
                    last = nc.tensor.transpose(ps_m[0][:, j * P:(j + 1) * P], zT[:, j * P:(j + 1) * P], ident[:, :])
                last.then_inc(zT_ps, 1)

            pe.wait_ge(vexp_ones, 2 * Q4)
            pe.wait_ge(w_late_in, 48)
            both_phases_loop(pe, attend)
            last_s = Step(NS // 2 - 1, 1)
            pe.wait_ge(probT_ready, GROUPS)
            pe.wait_ge(attn_ready, GROUPS - 2)
            values(last_s, SB - 1)
            attn_transposes(last_s, NS)
            out_project(last_s)
            xn_transposes(Step(0, 0), 1)
            pe.wait_ge(x2_ready, NS - 1 + FREE)
            branch_transposes(last_s, NS)

            def up(s, first):
                pe.wait_ge(h_ready, s.t + 1 + NS)
                for c in range(FC):
                    if not first:
                        pe.wait_ge(hid_ready, s.t * FC - FC + c + 1)
                    nc.tensor.matmul(ps_ff[c][:, :], w1_sb[:, c * P:(c + 1) * P], hT[s.parity][:, :],
                                     start=True, stop=True).then_inc(ff_ps, 1)

            def branch2_transposes(s):
                pe.wait_ge(z2_ready, s.t + 1)
                pe.wait_ge(x2_ready, NS + FREE)
                pe.wait_ge(y_ready, s.t + FREE)
                for j in range(SB):
                    last = nc.tensor.transpose(ps_m[0][:, j * P:(j + 1) * P], zT[:, j * P:(j + 1) * P], ident[:, :])
                last.then_inc(z2T_ps, 1)

            def feed(s, first, final):
                up(s, first)
                if not first:
                    branch2_transposes(s.plus(-1))
                if not final:
                    if not first:
                        pe.wait_ge(h_scaled, s.t + NS)
                    xn_transposes(s.plus(1), 1)
                for c in range(FC):
                    pe.wait_ge(hid_ready, s.t * FC + c + 1)
                    last = nc.tensor.matmul(ps_o[0][:, :], w2_sb[:, c * D:(c + 1) * D], hid[:, c, :],
                                            start=(c == 0), stop=(c == FC - 1))
                last.then_inc(w2_ps, 1)

            pe.wait_ge(z_ready, NS + FREE)
            pe.wait_ge(attn_ready, GROUPS)
            both_phases_loop(pe, feed)
            branch2_transposes(last_s)

        @block.scalar
        def _(act):
            act.dma_start(wada_sb[:, :], W_ada).then_inc(w_ada_in, 16)
            act.dma_start(cond_sb[:, :], cond).then_inc(w_ada_in, 16)
            for dst, src in ((wk_sb, Wk), (wq_sb, Wq), (wv_in, Wv)):
                act.dma_start(dst[:, :], src).then_inc(w_qkv_in, 16)
            act.dma_start(wo_sb[:, :], Wo).then_inc(w_late_in, 16)
            act.dma_start(w1_sb[:, :], W1).then_inc(w_late_in, 16)
            act.dma_start(w2_sb[:, :].rearrange("p (c d) -> p c d", c=FC),
                          W2.rearrange("(c p) d -> p c d", p=P)).then_inc(w_late_in, 16)

            def with_bias(dst, bank, r, done):
                nc.scalar.activation(dst, bank[:, :], ACT.Identity, bias=biasT[:, r:r + 1]).then_inc(done, 1)

            def take_k(s, early=False):
                act.wait_ge(k_ps, s.t + 1)
                if not early:
                    act.wait_ge(kexp_in[s.parity], s.pair * KINC)
                with_bias(kT[s.parity][:, :], ps_m[1], K_B, k_ready)

            def take_q(s, early=False):
                act.wait_ge(q_ps, s.t + 1)
                if not early:
                    act.wait_ge(s_ps, s.t * SB - SB)
                with_bias(qT[s.parity][:, :], ps_m[0], Q_B, q_ready)

            def take_v(s):
                act.wait_ge(v_ps, s.t + 1)
                act.wait_ge(vx_ready, s.t)
                with_bias(vT[:, :], ps_m[0], V_B, v_ready)

            def place_v(s, h4, early=False):
                act.wait_ge(vx_ready, s.t + 1)
                if not early:
                    act.wait_ge(o_ps, s.t * SB - SB)
                rows = slice(h4 * N, (h4 + 1) * N)
                nc.scalar.activation(vexp[s.parity][rows, :, h4, :, 0:HD],
                                     vx[rows, :].rearrange("k (b g d) -> k b g d", b=BS, g=HQ),
                                     ACT.Copy).then_inc(vexp_ready, 1)

            def exps(n, j, early=False):
                act.wait_ge(dif_ready, n + 1)
                if not early:
                    act.wait_ge(probT_ps, n - 1)
                nc.scalar.activation(prob[j % 2][:, :], sdif[j % 2][:, :], ACT.Exp, scale=SCALE).then_inc(prob_ready, 1)

            def take_probT(n, j, early=False):
                act.wait_ge(probT_ps, n + 1)
                if not early:
                    act.wait_ge(o_ps, n - 1)
                nc.scalar.activation(probT[j % 2][:, :], ps_p[j % 2][:, :], ACT.Copy).then_inc(probT_ready, 1)

            def take_attnT(t):
                act.wait_ge(attnT_ps, t + 1 + FREE)
                act.wait_ge(wo_ps, t + FREE)
                nc.scalar.activation(attnT[:, :], ps_m[1][:, :], ACT.Copy).then_inc(attnT_ready, 1)

            act.wait_ge(setupT_copied, 1)
            s0 = Step(0, 0)
            take_k(s0, True)
            take_q(s0, True)
            act.wait_ge(vexp_zero, 2)
            take_v(s0)
            for h4 in range(Q4):
                place_v(s0, h4, True)
            exps(0, 0, True)

            def attend(s, first, final):
                for j in range(SB):
                    n = s.t * SB + j
                    if j == 1 and not final:
                        take_q(s.plus(1), first)
                    if j == 2 and not final:
                        take_v(s.plus(1))
                    take_probT(n, j, first and j < 2)
                    if j == 3 and not final:
                        place_v(s.plus(1), 0, first)
                        place_v(s.plus(1), 1, first)
                    if not (final and j == SB - 1):
                        exps(n + 1, j + 1, first and j == 0)
                    if j == 0 and not final:
                        take_k(s.plus(1), first)
                    if j == 1 and not first:
                        take_attnT(s.t - 1)
                    if j == 3 and not final:
                        place_v(s.plus(1), 2, first)
                        place_v(s.plus(1), 3, first)

            both_phases_loop(act, attend)
            take_attnT(NS - 1)

            def gelus(s, first, final):
                for c in range(FC):
                    act.wait_ge(ff_ps, s.t * FC + c + 1)
                    if not first:
                        act.wait_ge(w2_ps, s.t + FREE)
                    nc.scalar.activation(hid[:, c, :], ps_ff[c][:, :], ACT.Gelu,
                                         bias=biasT[:, F1_B + c:F1_B + c + 1]).then_inc(hid_ready, 1)

            both_phases_loop(act, gelus)

        @block.vector
        def _(dve):
            steps = [0]

            def ln_link(instruction):
                steps[0] += 1
                instruction.then_inc(ln_step, 1)
                dve.wait_ge(ln_step, steps[0])

            def group_stats(t, j):
                nc.vector.bn_stats(bn[:, bass.ds(t * SB + j, 1), :],
                                   x_sb[:, bass.ds(t * T + j * D, D)]).then_inc(bn_done, 1)

            def combine(ln, c0, c1):
                c = slice(c0, c1)
                me, m2e, mo, m2o = (bn[:, c, i] for i in (1, 2, 4, 5))
                nc.vector.tensor_tensor(mean[ln][:, c], me, mo, ALU.add).then_inc(ln_step, 1)
                nc.vector.tensor_tensor(ln_dif[:, c], me, mo, ALU.subtract).then_inc(ln_step, 1)
                steps[0] += 2
                ln_link(nc.vector.tensor_tensor(ln_m2[:, c], m2e, m2o, ALU.add))
                nc.vector.tensor_scalar(mean[ln][:, c], mean[ln][:, c], 0.5, None, ALU.mult).then_inc(ln_step, 1)
                nc.vector.scalar_tensor_tensor(ln_sq[:, c], ln_dif[:, c], 0.25, ln_dif[:, c], ALU.mult,
                                               ALU.mult).then_inc(ln_step, 1)
                steps[0] += 2
                ln_link(nc.vector.tensor_scalar(ln_m2[:, c], ln_m2[:, c], 1.0 / D, EPS, ALU.mult, ALU.add))
                nc.vector.tensor_tensor(ln_var[:, c], ln_m2[:, c], ln_sq[:, c], ALU.add).then_inc(ln_ready, 1)

            def scale_h(s, ln, early=False):
                n = ln * NS
                dve.wait_ge(xnT_ps, s.t + 1 + n)
                if ln:
                    dve.wait_ge(ff_ps, s.t * FC - FC)
                elif not early:
                    dve.wait_ge(v_ps, s.t - 1)
                bank = ps_p[s.parity] if ln else ps_m[0]
                nc.vector.tensor_tensor(per_batch(hT[s.parity][:, :]), per_batch(bank[:, :]),
                                        ada(SCALE2 if ln else SCALE1, s.t), ALU.mult).then_inc(h_scaled, 1)

            def v_blocks(s):
                dve.wait_ge(v_ready, s.t + 1)
                dve.wait_ge(vexp_ready, s.t * Q4)
                nc.vector.transpose(vx[:, :], vT[:, :]).then_inc(vx_ready, 1)

            def less_max(n, j, early=False):
                heads = ps_s[j % 2][:, :].rearrange("p (h k) -> p h k", h=H)
                dve.wait_ge(s_ps, n + 1)
                if not early:
                    dve.wait_ge(dif_ready, n - 1)
                nc.vector.tensor_reduce(smax[j % 2][:, :], heads, axis=AX.X, op=ALU.max).then_inc(max_ready, 1)
                dve.wait_ge(max_ready, n + 1)
                if not early:
                    dve.wait_ge(prob_ready, n - 1)
                nc.vector.tensor_tensor(sdif[j % 2][:, :].rearrange("p (h k) -> p h k", h=H), heads,
                                        smax[j % 2][:, :].unsqueeze(2).to_broadcast([P, H, N]),
                                        ALU.subtract).then_inc(dif_ready, 1)

            def normalize_heads(s, j, n, early):
                heads = ps_o[j % 2][:, 0:H * VW].rearrange("p (h w) -> p h w", w=VW)
                dve.wait_ge(o_ps, n + 1)
                if not early:
                    dve.wait_ge(attn_ready, n - 1)
                nc.vector.reciprocal(rsum[j % 2][:, :].unsqueeze(2), heads[:, :, HD:VW]).then_inc(rsum_ready, 1)
                dve.wait_ge(rsum_ready, n + 1)
                if j == 0 and not early:
                    dve.wait_ge(attnT_ps, s.t - 1 + FREE)
                nc.vector.tensor_tensor(attn[s.parity][:, j, :].rearrange("p (h d) -> p h d", d=HD),
                                        heads[:, :, 0:HD], rsum[j % 2][:, :].unsqueeze(2).to_broadcast([P, H, HD]),
                                        ALU.mult).then_inc(attn_ready, 1)

            def gate(s, r, bias, bank, ps_done, zT_read, done):
                dve.wait_ge(ps_done, s.t + 1 + FREE)
                dve.wait_ge(zT_read, s.t + FREE)
                nc.vector.scalar_tensor_tensor(per_batch(zT[:, :]), per_batch(bank[:, :]), biasT[:, bias:bias + 1],
                                               ada(r, s.t), ALU.add, ALU.mult).then_inc(done, 1)

            def add_branch(s, ps_done, done):
                dve.wait_ge(ps_done, s.t + 1 + FREE)
                nc.vector.tensor_tensor(tokens(s.t), ps_m[0][:, :], tokens(s.t), ALU.add).then_inc(done, 1)

            for done in (x2_ready, z_ready, y_ready):
                dve.sem_inc(done, FREE)
            dve.memset(kexp[0][:, 0:H // 2, :], 0.0).then_inc(kexp_zero, 1)
            dve.wait_ge(x_in[0], 16)
            for j in range(SB):
                group_stats(0, j)
            dve.wait_ge(bn_done, SB)
            combine(0, 0, SB)
            dve.wait_ge(setupT_ready, 1)
            nc.vector.tensor_copy(biasT[:, :], ps_m[0][:, 0:15]).then_inc(setupT_copied, 1)
            dve.wait_ge(setupT_ready, 2)
            nc.vector.tensor_copy(condT[:, :], ps_m[1][:, 0:P]).then_inc(setupT_copied, 1)
            dve.wait_ge(setupT_copied, 2)
            for r in range(6):
                bank, c = ps_o[r // 4], r % 4 * B
                dve.wait_ge(ada_ps, 4 if r < 4 else 6)
                nc.vector.tensor_scalar(adaT[:, r, :], bank[:, c:c + B], biasT[:, ADA_B + r:ADA_B + r + 1],
                                        1.0 if r in (SCALE1, SCALE2) else 0.0, ALU.add, ALU.add).then_inc(ada_ready, 1)
            dve.wait_ge(ada_ready, 6)
            scale_h(Step(0, 0), 0, True)
            for t in range(1, NS):
                dve.wait_ge(x_in[t], 16)
            with dve.Fori(1, NS) as t:
                for j in range(SB):
                    group_stats(t, j)
            dve.wait_ge(bn_done, GROUPS)
            combine(0, SB, GROUPS)
            v_blocks(Step(0, 0))
            less_max(0, 0, True)

            def attend(s, first, final):
                for j in range(SB):
                    n = s.t * SB + j
                    if not (final and j == SB - 1):
                        less_max(n + 1, j + 1, first and j == 0)
                    if j == 0 and not final:
                        scale_h(s.plus(1), 0, first)
                    if j == 3 and not first:
                        gate(s.plus(-1), GATE1, O_B, ps_m[1], wo_ps, zT_ps, z_ready)
                    if not (first and j == 0):
                        before = s if j else s.plus(-1)
                        normalize_heads(before, (j - 1) % SB, n - 1, first and j < 3)
                    if j == 2 and not final:
                        v_blocks(s.plus(1))
                    if j == 3 and not first:
                        add_branch(s.plus(-1), zT_ps, x2_ready)
                        dve.wait_ge(x2_ready, s.t + FREE)
                        for g in range(SB):
                            group_stats(s.plus(-1).t, g)
                    if final and j == 0:
                        dve.wait_ge(bn_done, GROUPS + (NS - 2) * SB)
                        dve.wait_ge(rstd_ready, 2)
                        combine(1, 0, (NS - 2) * SB)

            both_phases_loop(dve, attend)
            last_s = Step(NS // 2 - 1, 1)
            normalize_heads(last_s, SB - 1, GROUPS - 1, False)
            gate(last_s, GATE1, O_B, ps_m[1], wo_ps, zT_ps, z_ready)
            scale_h2_first = Step(0, 0)
            dve.wait_ge(xnT_ps, 1 + NS)
            nc.vector.tensor_tensor(per_batch(hT[0][:, :]), per_batch(ps_p[0][:, :]), ada(SCALE2, 0),
                                    ALU.mult).then_inc(h_scaled, 1)
            add_branch(last_s, zT_ps, x2_ready)
            dve.wait_ge(x2_ready, NS + FREE)
            for g in range(SB):
                group_stats(last_s.t, g)
            dve.wait_ge(bn_done, 2 * GROUPS)
            dve.wait_ge(rstd_ready, 3)
            combine(1, (NS - 2) * SB, GROUPS)

            def feed(s, first, final):
                if not first:
                    gate(s.plus(-1), GATE2, F2_B, ps_o[0], w2_ps, z2T_ps, z2_ready)
                    add_branch(s.plus(-1), z2T_ps, y_ready)
                if not final:
                    scale_h(s.plus(1), 1)

            both_phases_loop(dve, feed)
            gate(last_s, GATE2, F2_B, ps_o[0], w2_ps, z2T_ps, z2_ready)
            add_branch(last_s, z2T_ps, y_ready)


_INS = ['x', 'cond_1024', 'L0_cond_W_ada', 'L0_cond_b_ada', 'L0_cond_Wq', 'L0_cond_bq', 'L0_cond_Wk', 'L0_cond_bk',
        'L0_cond_Wv', 'L0_cond_bv', 'L0_cond_Wo', 'L0_cond_bo', 'L0_cond_W1', 'L0_cond_b1', 'L0_cond_W2',
        'L0_cond_b2']


def kernel(**inputs):
    import numpy as _np
    import concourse.bacc as _bacc
    from concourse import mybir as _mybir
    from concourse.bass_utils import run_bass_kernel_spmd as _run

    nc = _bacc.Bacc("TRN2", target_bir_lowering=False, num_devices=1)
    arrays, args = {}, []
    for name in _INS:
        a = _np.ascontiguousarray(inputs[name])
        arrays[f"in_{name}_dram"] = a
        args.append(nc.dram_tensor(f"in_{name}_dram", a.shape, _mybir.dt.from_np(a.dtype), kind="ExternalInput").ap())
    shape = inputs["x"].shape
    args.append(nc.dram_tensor("out_0_dram", shape, _mybir.dt.float32, kind="ExternalOutput").ap())
    dit_block(nc, *args)
    r = _run(nc, [arrays], core_ids=[0])
    return r.results[0]["out_0_dram"]
```

```python
from contextlib import ExitStack

import concourse.bass as bass
from concourse import mybir

F32 = mybir.dt.float32
ALU = mybir.AluOpType
ACT = mybir.ActivationFunctionType
AX = mybir.AxisListType


class Step:

    def __init__(self, pair, parity):
        self.pair, self.parity = pair, parity
        self.t = pair * 2 + parity

    def plus(self, d):
        parity = (self.parity + d) % 2
        return Step(self.pair + (self.parity + d - parity) // 2, parity)


def dit_block(nc, x, cond, W_ada, b_ada, Wq, bq, Wk, bk, Wv, bv, Wo, bo, W1, b1, W2, b2, out):
    B, N, D = x.shape
    P = 128
    HD = 8
    H = D // HD
    Q4 = 4
    HQ = H // Q4
    FF = W1.shape[1]
    FC = FF // P
    GROUPS = B // Q4
    SB = 4
    T = SB * P
    NS = GROUPS // SB
    BS = SB * Q4
    VW = HD + 1
    EPS = 1e-05
    SCALE = float(1.0 / (HD ** 0.5))
    KINC = 16 * HQ
    FREE = 1
    assert N == 32 and D == P and B % (Q4 * SB) == 0 and NS % 2 == 0

    with ExitStack() as ctx:
        def sb(name, shape):
            return ctx.enter_context(nc.sbuf_tensor(name, shape, F32))

        def pb(name):
            return ctx.enter_context(nc.psum_tensor(name, [P, T], F32))

        def sem(name):
            return ctx.enter_context(nc.semaphore(name))

        x_sb = sb("x_sb", [P, NS * T])
        wada_sb = sb("wada_sb", [P, 6 * D])
        cond_sb = sb("cond_sb", [B, D])
        condT = sb("condT", [D, B])
        wq_sb, wk_sb, wv_in, wv_sb, wo_sb = (sb(n, [P, D]) for n in ("wq_sb", "wk_sb", "wv_in", "wv_sb", "wo_sb"))
        w1_sb = sb("w1_sb", [P, FF])
        w2_sb = sb("w2_sb", [P, FC * D])
        bias_rows = [sb(f"bias_rows{i}", [P, P]) for i in range(2)]
        NB0, NB1 = 9, 2 + FC
        biasT = sb("biasT", [P, NB0 + NB1])
        ADA_B, Q_B, K_B, V_B, O_B, F2_B, F1_B = 0, 6, 7, 8, NB0, NB0 + 1, NB0 + 2
        kmask = sb("kmask", [P, Q4])
        kbias = sb("kbias", [P, Q4])
        adaT = sb("adaT", [D, 6, B])
        ident = sb("ident", [P, P])
        minus_half = sb("minus_half", [P, GROUPS])
        bn = sb("bn", [P, GROUPS, 6])
        mean = [sb(f"mean{i}", [P, GROUPS]) for i in (1, 2)]
        rstd = [sb(f"rstd{i}", [P, GROUPS]) for i in (1, 2)]
        ln_dif, ln_m2, ln_sq, ln_var = (sb(n, [P, GROUPS]) for n in ("ln_dif", "ln_m2", "ln_sq", "ln_var"))
        xn = [sb(f"xn{i}", [P, T]) for i in range(2)]
        hT = [sb(f"hT{i}", [D, T]) for i in range(2)]
        qT = [sb(f"qT{i}", [P, T]) for i in range(2)]
        kTm = sb("kTm", [P, Q4, T])
        vT = sb("vT", [P, T])
        vx = sb("vx", [P, T])
        kexp = [sb(f"kexp{i}", [P, H, T]) for i in range(2)]
        vexp = [sb(f"vexp{i}", [P, BS, Q4, HQ, VW]) for i in range(2)]
        smax = [sb(f"smax{i}", [P, H]) for i in range(2)]
        sdif = [sb(f"sdif{i}", [P, H * N]) for i in range(2)]
        prob = [sb(f"prob{i}", [P, H * N]) for i in range(2)]
        probT = [sb(f"probT{i}", [P, H * N]) for i in range(2)]
        rsum = [sb(f"rsum{i}", [P, H]) for i in range(2)]
        attn = [sb(f"attn{i}", [P, SB, D]) for i in range(2)]
        attnT = sb("attnT", [P, T])
        zT = sb("zT", [D, T])
        hid = sb("hid", [P, FC, T])

        ps_s = [pb("ps_s0"), pb("ps_s1")]
        ps_p = [pb("ps_p0"), pb("ps_p1")]
        ps_o = [pb("ps_o0"), pb("ps_o1")]
        ps_m = [pb("ps_m0"), pb("ps_m1")]
        ps_ff = [ps_s[0], ps_s[1], ps_o[1], ps_p[1]]

        x_in = [sem(f"x_in{t}") for t in range(NS)]
        (w_ada_in, w_qkv_in, w_late_in) = map(sem, ("w_ada_in", "w_qkv_in", "w_late_in"))
        rows_in = [sem(f"rows_in{i}") for i in range(2)]
        (rows_zero, id_zero, id_ready, consts_ready, vexp_zero, vexp_ones, wv_ready) = map(sem, (
            "rows_zero", "id_zero", "id_ready", "consts_ready", "vexp_zero", "vexp_ones", "wv_ready"))
        kexp_zero = [sem(f"kexp_zero{i}") for i in range(2)]
        (setupT_ready, setupT_copied, ada_ps, ada_ready, kmask_ready, kbias_ready, table_loaded) = map(sem, (
            "setupT_ready", "setupT_copied", "ada_ps", "ada_ready", "kmask_ready", "kbias_ready", "table_loaded"))
        (bn_done, ln_step, ln_ready, rstd_ready, xn_sub, xn_ready) = map(sem, (
            "bn_done", "ln_step", "ln_ready", "rstd_ready", "xn_sub", "xn_ready"))
        (xnT_ps, h_scaled, h_ready) = map(sem, ("xnT_ps", "h_scaled", "h_ready"))
        (q_ps, k_ps, v_ps, q_ready, k_ready, v_ready, vx_ready, vexp_ready) = map(sem, (
            "q_ps", "k_ps", "v_ps", "q_ready", "k_ready", "v_ready", "vx_ready", "vexp_ready"))
        kexp_in = [sem(f"kexp_in{i}") for i in range(2)]
        (s_ps, max_ready, dif_ready, prob_ready, probT_ps, probT_ready, o_ps, rsum_ready, attn_ready) = map(sem, (
            "s_ps", "max_ready", "dif_ready", "prob_ready", "probT_ps", "probT_ready", "o_ps", "rsum_ready",
            "attn_ready"))
        (attnT_ps, attnT_ready, wo_ps, z_ready, zT_ps, x2_ready) = map(sem, (
            "attnT_ps", "attnT_ready", "wo_ps", "z_ready", "zT_ps", "x2_ready"))
        (ff_ps, hid_ready, w2_ps, z2_ready, z2T_ps, y_ready, y_out) = map(sem, (
            "ff_ps", "hid_ready", "w2_ps", "z2_ready", "z2T_ps", "y_ready", "y_out"))

        def tokens(t):
            return x_sb[:, bass.ds(t * T, T)]

        def ada(r, t):
            return adaT[:, r, bass.ds(t * BS, BS)].unsqueeze(2).to_broadcast([D, BS, N])

        def per_batch(ap):
            return ap.rearrange("p (b q) -> p b q", q=N)

        def per_group(stat, t):
            return stat[:, bass.ds(t * SB, SB)].unsqueeze(2).to_broadcast([P, SB, D])

        SHIFT1, SCALE1, GATE1, SHIFT2, SCALE2, GATE2 = range(6)
        block = ctx.enter_context(nc.Block())

        def both_phases_loop(eng, body):
            body(Step(0, 0), True, False)
            with eng.Fori(0, (NS - 2) // 2) as i:
                body(Step(i, 1), False, False)
                body(Step(i + 1, 0), False, False)
            body(Step(NS // 2 - 1, 1), False, True)

        @block.sync
        def _(sp):
            def load_x(t):
                sp.dma_start(x_sb[:, t * T:(t + 1) * T].rearrange("p (g d) -> p g d", g=SB),
                             x[t * BS:(t + 1) * BS].rearrange("(g b) q d -> (b q) g d", g=SB)).then_inc(x_in[t], 16)

            def load_row(i, src, r, n):
                sp.dma_start(bias_rows[i][r:r + n, :], src.rearrange("(r p) -> r p", p=P)).then_inc(rows_in[i], 16)

            load_x(0)
            sp.wait_ge(rows_zero, 2)
            load_row(0, b_ada, ADA_B, 6)
            load_row(0, bk, K_B, 1)
            load_row(0, bq, Q_B, 1)
            sp.dma_start(bias_rows[0][V_B:V_B + 1, :].rearrange("o (h g d) -> o h g d", h=Q4, g=HQ),
                         bv.rearrange("(o g h d) -> o h g d", o=1, g=HQ, h=Q4)).then_inc(rows_in[0], 16)
            load_x(1)
            load_x(2)
            load_row(1, bo, 0, 1)
            load_row(1, b2, 1, 1)
            load_row(1, b1, 2, FC)
            for t in range(3, NS):
                load_x(t)

            def expand_k(s, early=False):
                sp.wait_ge(k_ready, s.t + 1)
                if not early:
                    sp.wait_ge(s_ps, s.t * SB - SB)
                for g in range(HQ):
                    rows = slice(g * Q4 * HD, (g + 1) * Q4 * HD)
                    sp.dma_start(kexp[s.parity][rows, g * Q4:(g + 1) * Q4, :],
                                 kTm[rows, :, :]).then_inc(kexp_in[s.parity], 16)

            for t in range(2):
                sp.wait_ge(kexp_zero[t], 2)
                expand_k(Step(0, t), True)
            with sp.Fori(1, NS // 2) as i:
                expand_k(Step(i, 0))
                expand_k(Step(i, 1))
            with sp.Fori(0, NS) as t:
                sp.wait_ge(y_ready, t + 1 + FREE)
                sp.dma_start(out[bass.ds(t * BS, BS)].rearrange("(g b) q d -> (b q) g d", g=SB),
                             tokens(t).rearrange("p (g d) -> p g d", g=SB)).then_inc(y_out, 16)
            sp.wait_ge(y_out, 16 * NS)

        @block.gpsimd
        def _(pool):
            for i in range(2):
                pool.memset(bias_rows[i][:, :], 0.0).then_inc(rows_zero, 1)
            pool.memset(ident[:, :], 0.0).then_inc(id_zero, 1)
            pool.memset(minus_half[:, :], -0.5).then_inc(consts_ready, 1)
            pool.wait_ge(id_zero, 1)
            pool.affine_select(out=ident[:, :], in_=ident[:, :], compare_op=ALU.not_equal, fill=1.0, base=0,
                               pattern=[[-1, P]], channel_multiplier=1).then_inc(id_ready, 1)

            def rstd_of(ln, c0, c1, count):
                pool.wait_ge(ln_ready, count)
                pool.tensor_tensor(rstd[ln][:, c0:c1], ln_var[:, c0:c1], minus_half[:, c0:c1],
                                   ALU.pow).then_inc(rstd_ready, 1)

            def normalize(s, ln, unused=False):
                n = ln * NS
                if not unused:
                    pool.wait_ge(xnT_ps, s.t - 1 + n)
                pool.wait_ge(consts_ready, 1)
                x3 = tokens(s.t).rearrange("p (g d) -> p g d", g=SB)
                xn3 = xn[s.parity][:, :].rearrange("p (g d) -> p g d", g=SB)
                nc.gpsimd.tensor_tensor(xn3, x3, per_group(mean[ln], s.t), ALU.subtract).then_inc(xn_sub, 1)
                pool.wait_ge(xn_sub, s.t + 1 + n)
                pool.wait_ge(consts_ready, 1)
                nc.gpsimd.tensor_tensor(xn3, xn3, per_group(rstd[ln], s.t), ALU.mult).then_inc(xn_ready, 1)

            def shift(s, ln):
                n = ln * NS
                pool.wait_ge(h_scaled, s.t + 1 + n)
                pool.wait_ge(consts_ready, 1)
                h = per_batch(hT[s.parity][:, :])
                nc.gpsimd.tensor_tensor(h, h, ada(SHIFT2 if ln else SHIFT1, s.t), ALU.add).then_inc(h_ready, 1)

            pool.wait_ge(consts_ready, 1)
            rstd_of(0, 0, SB, 1)
            pool.wait_ge(rstd_ready, 1)
            normalize(Step(0, 0), 0, True)
            pool.wait_ge(w_qkv_in, 48)
            pool.tensor_copy(wv_sb[:, :].rearrange("p (h g d) -> p h g d", h=Q4, g=HQ),
                             wv_in[:, :].rearrange("p (g h d) -> p h g d", h=Q4, g=HQ)).then_inc(wv_ready, 1)
            shift(Step(0, 0), 0)
            pool.memset(kexp[0][:, H // 2:H, :], 0.0).then_inc(kexp_zero[0], 1)
            rstd_of(0, SB, 2 * SB, 2)
            pool.wait_ge(rstd_ready, 2)
            normalize(Step(0, 1), 0, True)
            for p in range(2):
                pool.memset(vexp[p][:, :, :, :, :], 0.0).then_inc(vexp_zero, 1)
            pool.wait_ge(vexp_zero, 2)
            for p in range(2):
                for h4 in range(Q4):
                    pool.memset(vexp[p][32 * h4:32 * h4 + 32, :, h4, :, HD:VW], 1.0).then_inc(vexp_ones, 1)
            pool.wait_ge(vexp_ones, 2 * Q4)
            shift(Step(0, 1), 0)
            rstd_of(0, 2 * SB, 3 * SB, 3)
            pool.wait_ge(rstd_ready, 3)
            normalize(Step(1, 0), 0)
            rstd_of(0, 3 * SB, GROUPS, 4)
            pool.wait_ge(rstd_ready, 4)
            normalize(Step(1, 1), 0)
            with pool.Fori(1, NS // 2 - 1) as i:
                for parity in range(2):
                    shift(Step(i, parity), 0)
                    normalize(Step(i + 1, parity), 0)
            shift(Step(NS // 2 - 1, 0), 0)
            shift(Step(NS // 2 - 1, 1), 0)
            rstd_of(1, 0, (NS - 2) * SB, 5)
            pool.wait_ge(rstd_ready, 5)
            normalize(Step(0, 0), 1)
            normalize(Step(0, 1), 1)
            shift(Step(0, 0), 1)
            normalize(Step(1, 0), 1)
            shift(Step(0, 1), 1)
            rstd_of(1, (NS - 2) * SB, GROUPS, 6)
            pool.wait_ge(rstd_ready, 6)
            normalize(Step(1, 1), 1)
            with pool.Fori(1, NS // 2 - 1) as i:
                for parity in range(2):
                    shift(Step(i, parity), 1)
                    normalize(Step(i + 1, parity), 1)
            shift(Step(NS // 2 - 1, 0), 1)
            shift(Step(NS // 2 - 1, 1), 1)

        @block.tensor
        def _(pe):
            for done in (attnT_ps, wo_ps, zT_ps, w2_ps, z2T_ps):
                pe.sem_inc(done, FREE)

            def xn_transposes(s, ln):
                pe.wait_ge(xn_ready, s.t + 1 + ln * NS)
                bank = ps_p[0] if ln else ps_m[0]
                for j in range(SB):
                    last = nc.tensor.transpose(bank[:, j * P:(j + 1) * P], xn[s.parity][:, j * P:(j + 1) * P],
                                               ident[:, :])
                last.then_inc(xnT_ps, 1)

            def project(s, w, bank, done):
                nc.tensor.matmul(bank[:, :], w[:, :], hT[s.parity][:, :], start=True, stop=True).then_inc(done, 1)

            def scores(s, j):
                for b in range(Q4):
                    q = slice(j * P + b * N, j * P + (b + 1) * N)
                    last = nc.tensor.matmul(ps_s[j % 2][b * N:(b + 1) * N, :], qT[s.parity][:, q],
                                            kexp[s.parity][:, :, q], start=True, stop=True)
                last.then_inc(s_ps, 1)

            def prob_transposes(j):
                for g in range(HQ):
                    c = slice(g * P, (g + 1) * P)
                    last = nc.tensor.transpose(ps_p[j % 2][:, c], prob[j % 2][:, c], ident[:, :])
                last.then_inc(probT_ps, 1)

            def values(s, j):
                for b in range(Q4):
                    for g in range(HQ):
                        o = g * Q4 * VW
                        last = nc.tensor.matmul(ps_o[j % 2][b * N:(b + 1) * N, o:o + Q4 * VW],
                                                probT[j % 2][:, g * P + b * N:g * P + (b + 1) * N],
                                                vexp[s.parity][:, j * Q4 + b, :, g, :], start=True, stop=True)
                last.then_inc(o_ps, 1)

            pe.wait_ge(id_ready, 1)
            pe.wait_ge(w_ada_in, 32)
            nc.tensor.transpose(ps_m[1][:, 0:P], cond_sb[:, :], ident[:, :]).then_inc(setupT_ready, 1)
            pe.wait_ge(rows_in[0], 16 * 4)
            nc.tensor.transpose(ps_p[0][:, 0:P], bias_rows[0][:, :], ident[:, :]).then_inc(setupT_ready, 1)
            pe.wait_ge(setupT_copied, 1)

            def condition(r, bank):
                nc.tensor.matmul(bank[:, :B], wada_sb[:, r * D:(r + 1) * D], condT[:, :],
                                 start=True, stop=True).then_inc(ada_ps, 1)

            condition(SCALE1, ps_o[0])
            condition(SHIFT1, ps_o[1])
            xn_transposes(Step(0, 0), 0)
            condition(GATE1, ps_s[0])
            condition(SHIFT2, ps_s[1])
            pe.wait_ge(ada_ready, 2)
            condition(SCALE2, ps_o[0])
            condition(GATE2, ps_o[1])
            pe.wait_ge(h_ready, 1)
            pe.wait_ge(w_qkv_in, 48)
            project(Step(0, 0), wk_sb, ps_m[1], k_ps)
            project(Step(0, 0), wq_sb, ps_m[0], q_ps)
            pe.wait_ge(wv_ready, 1)
            pe.wait_ge(q_ready, 1)
            project(Step(0, 0), wv_sb, ps_m[0], v_ps)
            pe.wait_ge(rows_in[1], 16 * 3)
            nc.tensor.transpose(ps_p[1][:, 0:P], bias_rows[1][:, :], ident[:, :]).then_inc(setupT_ready, 1)
            pe.wait_ge(ada_ready, 6)
            pe.wait_ge(setupT_copied, 3)
            pe.wait_ge(vexp_ones, 2 * Q4)
            pe.wait_ge(w_late_in, 48)

            def attend(s, first, final):
                for j in range(SB):
                    n = s.t * SB + j
                    if j == 0:
                        pe.wait_ge(q_ready, s.t + 1)
                        pe.wait_ge(kexp_in[s.parity], (s.pair + 1) * KINC)
                    if not (first and j < 2):
                        pe.wait_ge(dif_ready, n - 1)
                    scores(s, j)
                    if j == 0 and not final:
                        if first:
                            pe.wait_ge(v_ready, 1)
                        else:
                            pe.wait_ge(x2_ready, s.t - 1 + FREE)
                        xn_transposes(s.plus(1), 0)
                    if j == 1 and not final:
                        pe.wait_ge(h_scaled, s.t + 2)
                        project(s.plus(1), wq_sb, ps_m[0], q_ps)
                    if j == 2 and not final:
                        pe.wait_ge(q_ready, s.t + 2)
                        project(s.plus(1), wv_sb, ps_m[0], v_ps)
                    if j == 3 and not first:
                        out_project(s.plus(-1))
                    if not (first and j == 0):
                        pe.wait_ge(prob_ready, n)
                        if not (first and j < 3):
                            pe.wait_ge(probT_ready, n - 2)
                        prob_transposes((j - 1) % SB)
                    if not (first and j < 2):
                        before = s if j > 1 else s.plus(-1)
                        pe.wait_ge(probT_ready, n - 1)
                        pe.wait_ge(vexp_ready, before.t * Q4 + Q4)
                        if not (first and j < 4):
                            pe.wait_ge(attn_ready, n - 3)
                        values(before, (j - 2) % SB)
                    if j == 0 and not final:
                        pe.wait_ge(h_ready, s.t + 2)
                        if first:
                            pe.wait_ge(k_ready, 1)
                        else:
                            pe.wait_ge(z_ready, s.t - 1 + FREE)
                        project(s.plus(1), wk_sb, ps_m[1], k_ps)
                    if j == 2 and not first:
                        attn_transposes(s.plus(-1), NS if final else s.t + 2)
                    if j == 3 and not first:
                        branch_transposes(s.plus(-1), NS if final else s.t + 2)

            def attn_transposes(s, k_read):
                pe.wait_ge(attn_ready, s.t * SB + SB)
                pe.wait_ge(k_ready, k_read)
                for j in range(SB):
                    last = nc.tensor.transpose(ps_m[1][:, j * P:(j + 1) * P], attn[s.parity][:, j, :], ident[:, :])
                last.then_inc(attnT_ps, 1)

            def out_project(s):
                pe.wait_ge(attnT_ready, s.t + 1)
                nc.tensor.matmul(ps_m[1][:, :], wo_sb[:, :], attnT[:, :], start=True, stop=True).then_inc(wo_ps, 1)

            def branch_transposes(s, v_read):
                pe.wait_ge(v_ready, v_read)
                pe.wait_ge(z_ready, s.t + 1 + FREE)
                for j in range(SB):
                    last = nc.tensor.transpose(ps_m[0][:, j * P:(j + 1) * P], zT[:, j * P:(j + 1) * P], ident[:, :])
                last.then_inc(zT_ps, 1)

            both_phases_loop(pe, attend)

            def up(s, c, first):
                if c == 0:
                    pe.wait_ge(h_ready, s.t + 1 + NS)
                if not first:
                    pe.wait_ge(hid_ready, s.t * FC - FC + c + 1)
                nc.tensor.matmul(ps_ff[c][:, :], w1_sb[:, c * P:(c + 1) * P], hT[s.parity][:, :],
                                 start=True, stop=True).then_inc(ff_ps, 1)

            last_s = Step(NS // 2 - 1, 1)
            s0 = Step(0, 0)
            pe.wait_ge(prob_ready, GROUPS)
            pe.wait_ge(probT_ready, GROUPS - 2)
            prob_transposes(SB - 1)
            pe.wait_ge(probT_ready, GROUPS - 1)
            pe.wait_ge(attn_ready, GROUPS - 3)
            values(last_s, SB - 2)
            xn_transposes(s0, 1)
            pe.wait_ge(probT_ready, GROUPS)
            pe.wait_ge(attn_ready, GROUPS - 2)
            values(last_s, SB - 1)
            pe.wait_ge(dif_ready, GROUPS)
            up(s0, 0, True)
            up(s0, 1, True)
            attn_transposes(last_s, NS)
            up(s0, 2, True)
            out_project(last_s)
            up(s0, 3, True)
            pe.wait_ge(h_scaled, NS + 1)
            xn_transposes(s0.plus(1), 1)
            pe.wait_ge(x2_ready, NS - 1 + FREE)
            branch_transposes(last_s, NS)

            def branch2_transposes(s):
                pe.wait_ge(z2_ready, s.t + 1 + FREE)
                pe.wait_ge(x2_ready, NS + FREE)
                pe.wait_ge(y_ready, s.t + FREE)
                for j in range(SB):
                    last = nc.tensor.transpose(ps_m[0][:, j * P:(j + 1) * P], zT[:, j * P:(j + 1) * P], ident[:, :])
                last.then_inc(z2T_ps, 1)

            def feed(s, first, final):
                if not first:
                    for c in range(FC):
                        up(s, c, False)
                    branch2_transposes(s.plus(-1))
                    if not final:
                        pe.wait_ge(h_scaled, s.t + 1 + NS)
                        xn_transposes(s.plus(1), 1)
                for c in range(FC):
                    pe.wait_ge(hid_ready, s.t * FC + c + 1)
                    if c == 0 and not first:
                        pe.wait_ge(z2_ready, s.t + FREE)
                    last = nc.tensor.matmul(ps_o[0][:, :], w2_sb[:, c * D:(c + 1) * D], hid[:, c, :],
                                            start=(c == 0), stop=(c == FC - 1))
                last.then_inc(w2_ps, 1)

            both_phases_loop(pe, feed)
            branch2_transposes(last_s)

        @block.scalar
        def _(act):
            act.dma_start(wada_sb[:, :], W_ada).then_inc(w_ada_in, 16)
            act.dma_start(cond_sb[:, :], cond).then_inc(w_ada_in, 16)
            for dst, src in ((wk_sb, Wk), (wq_sb, Wq), (wv_in, Wv)):
                act.dma_start(dst[:, :], src).then_inc(w_qkv_in, 16)
            act.dma_start(wo_sb[:, :], Wo).then_inc(w_late_in, 16)
            act.dma_start(w1_sb[:, :], W1).then_inc(w_late_in, 16)
            act.dma_start(w2_sb[:, :].rearrange("p (c d) -> p c d", c=FC),
                          W2.rearrange("(c p) d -> p c d", p=P)).then_inc(w_late_in, 16)

            act.wait_ge(consts_ready, 1)
            nc.scalar.activation(prob[0][:, 0:1], minus_half[:, 0:1], ACT.Exp).then_inc(table_loaded, 1)

            def with_bias(dst, bank, r, done):
                nc.scalar.activation(dst, bank[:, :], ACT.Identity, bias=biasT[:, r:r + 1]).then_inc(done, 1)

            def take_k(s, early=False):
                act.wait_ge(k_ps, s.t + 1)
                if not early:
                    before = s.plus(-1)
                    act.wait_ge(kexp_in[before.parity], (before.pair + 1) * KINC)
                for h4 in range(Q4):
                    last = nc.scalar.activation(kTm[:, h4, :], ps_m[1][:, :], ACT.Identity,
                                                scale=kmask[:, h4:h4 + 1], bias=kbias[:, h4:h4 + 1])
                last.then_inc(k_ready, 1)

            def take_q(s, early=False):
                act.wait_ge(q_ps, s.t + 1)
                if not early:
                    act.wait_ge(s_ps, s.t * SB - SB)
                with_bias(qT[s.parity][:, :], ps_m[0], Q_B, q_ready)

            def take_v(s, early=False):
                act.wait_ge(v_ps, s.t + 1)
                if not early:
                    act.wait_ge(vx_ready, s.t)
                with_bias(vT[:, :], ps_m[0], V_B, v_ready)

            def place_v(s, h4, early=False):
                act.wait_ge(vx_ready, s.t + 1)
                if not early:
                    act.wait_ge(o_ps, s.t * SB - SB)
                rows = slice(h4 * N, (h4 + 1) * N)
                nc.scalar.activation(vexp[s.parity][rows, :, h4, :, 0:HD],
                                     vx[rows, :].rearrange("k (b g d) -> k b g d", b=BS, g=HQ),
                                     ACT.Copy).then_inc(vexp_ready, 1)

            def exps(n, j, early=False):
                act.wait_ge(dif_ready, n + 1)
                if early:
                    act.wait_ge(table_loaded, 1)
                if not early:
                    act.wait_ge(probT_ps, n - 1)
                nc.scalar.activation(prob[j % 2][:, :], sdif[j % 2][:, :], ACT.Exp, scale=SCALE).then_inc(prob_ready, 1)

            def take_probT(n, j, early=False):
                act.wait_ge(probT_ps, n + 1)
                if not early:
                    act.wait_ge(o_ps, n - 1)
                nc.scalar.activation(probT[j % 2][:, :], ps_p[j % 2][:, :], ACT.Copy).then_inc(probT_ready, 1)

            def gelu(s, c, first):
                act.wait_ge(ff_ps, s.t * FC + c + 1)
                if not first:
                    act.wait_ge(w2_ps, s.t + FREE)
                nc.scalar.activation(hid[:, c, :], ps_ff[c][:, :], ACT.Gelu,
                                     bias=biasT[:, F1_B + c:F1_B + c + 1]).then_inc(hid_ready, 1)

            def take_attnT(t):
                act.wait_ge(attnT_ps, t + 1 + FREE)
                act.wait_ge(wo_ps, t + FREE)
                nc.scalar.activation(attnT[:, :], ps_m[1][:, :], ACT.Copy).then_inc(attnT_ready, 1)

            act.wait_ge(kbias_ready, 1)
            s0 = Step(0, 0)
            take_k(s0, True)
            take_q(s0, True)
            take_v(s0, True)
            act.wait_ge(vexp_zero, 2)
            for h4 in range(Q4):
                place_v(s0, h4, True)

            def attend(s, first, final):
                for j in range(SB):
                    n = s.t * SB + j
                    if j == 1 and not final:
                        take_q(s.plus(1), first)
                    if j == 2 and not final:
                        take_v(s.plus(1))
                    if not (first and j == 0):
                        take_probT(n - 1, (j - 1) % SB, first and j < 3)
                    if j == 3 and not final:
                        place_v(s.plus(1), 0, first)
                        place_v(s.plus(1), 1, first)
                    exps(n, j, first and j < 2)
                    if j == 0 and not final:
                        take_k(s.plus(1))
                    if j == 2 and not first:
                        take_attnT(s.t - 1)
                    if j == 3 and not final:
                        place_v(s.plus(1), 2, first)
                        place_v(s.plus(1), 3, first)

            both_phases_loop(act, attend)
            take_probT(GROUPS - 1, SB - 1)
            for c in range(FC):
                if c == 2:
                    take_attnT(NS - 1)
                gelu(s0, c, True)

            def gelus(s, first, final):
                if not first:
                    for c in range(FC):
                        gelu(s, c, False)

            both_phases_loop(act, gelus)

        @block.vector
        def _(dve):
            steps = [0]

            def ln_link(instruction):
                steps[0] += 1
                instruction.then_inc(ln_step, 1)
                dve.wait_ge(ln_step, steps[0])

            def group_stats(t, j):
                nc.vector.bn_stats(bn[:, bass.ds(t * SB + j, 1), :],
                                   x_sb[:, bass.ds(t * T + j * D, D)]).then_inc(bn_done, 1)

            def combine(ln, c0, c1):
                c = slice(c0, c1)
                me, m2e, mo, m2o = (bn[:, c, i] for i in (1, 2, 4, 5))
                nc.vector.tensor_tensor(mean[ln][:, c], me, mo, ALU.add).then_inc(ln_step, 1)
                nc.vector.tensor_tensor(ln_dif[:, c], me, mo, ALU.subtract).then_inc(ln_step, 1)
                steps[0] += 2
                ln_link(nc.vector.tensor_tensor(ln_m2[:, c], m2e, m2o, ALU.add))
                nc.vector.tensor_scalar(mean[ln][:, c], mean[ln][:, c], 0.5, None, ALU.mult).then_inc(ln_step, 1)
                nc.vector.scalar_tensor_tensor(ln_sq[:, c], ln_dif[:, c], 0.25, ln_dif[:, c], ALU.mult,
                                               ALU.mult).then_inc(ln_step, 1)
                steps[0] += 2
                ln_link(nc.vector.tensor_scalar(ln_m2[:, c], ln_m2[:, c], 1.0 / D, EPS, ALU.mult, ALU.add))
                nc.vector.tensor_tensor(ln_var[:, c], ln_m2[:, c], ln_sq[:, c], ALU.add).then_inc(ln_ready, 1)

            def scale_h(s, ln, early=False):
                n = ln * NS
                dve.wait_ge(xnT_ps, s.t + 1 + n)
                if ln and not early:
                    dve.wait_ge(ff_ps, s.t * FC - FC)
                elif not early:
                    dve.wait_ge(v_ps, s.t - 1)
                bank = ps_p[0] if ln else ps_m[0]
                nc.vector.tensor_tensor(per_batch(hT[s.parity][:, :]), per_batch(bank[:, :]),
                                        ada(SCALE2 if ln else SCALE1, s.t), ALU.mult).then_inc(h_scaled, 1)

            def v_blocks(s, early=False):
                dve.wait_ge(v_ready, s.t + 1)
                if not early:
                    dve.wait_ge(vexp_ready, s.t * Q4)
                nc.vector.transpose(vx[:, :], vT[:, :]).then_inc(vx_ready, 1)

            def less_max(n, j, early=False):
                heads = ps_s[j % 2][:, :].rearrange("p (h k) -> p h k", h=H)
                dve.wait_ge(s_ps, n + 1)
                if not early:
                    dve.wait_ge(dif_ready, n - 1)
                nc.vector.tensor_reduce(smax[j % 2][:, :], heads, axis=AX.X, op=ALU.max).then_inc(max_ready, 1)
                dve.wait_ge(max_ready, n + 1)
                if not early:
                    dve.wait_ge(prob_ready, n - 1)
                nc.vector.tensor_tensor(sdif[j % 2][:, :].rearrange("p (h k) -> p h k", h=H), heads,
                                        smax[j % 2][:, :].unsqueeze(2).to_broadcast([P, H, N]),
                                        ALU.subtract).then_inc(dif_ready, 1)

            def normalize_heads(s, j, n, early):
                heads = ps_o[j % 2][:, 0:H * VW].rearrange("p (h w) -> p h w", w=VW)
                dve.wait_ge(o_ps, n + 1)
                if not early:
                    dve.wait_ge(attn_ready, n - 1)
                nc.vector.reciprocal(rsum[j % 2][:, :].unsqueeze(2), heads[:, :, HD:VW]).then_inc(rsum_ready, 1)
                dve.wait_ge(rsum_ready, n + 1)
                if j == 0 and not early:
                    dve.wait_ge(attnT_ps, s.t - 1 + FREE)
                nc.vector.tensor_tensor(attn[s.parity][:, j, :].rearrange("p (h d) -> p h d", d=HD),
                                        heads[:, :, 0:HD], rsum[j % 2][:, :].unsqueeze(2).to_broadcast([P, H, HD]),
                                        ALU.mult).then_inc(attn_ready, 1)

            def gate(s, r, bias, bank, ps_done, zT_read, done):
                dve.wait_ge(ps_done, s.t + 1 + FREE)
                dve.wait_ge(zT_read, s.t + FREE)
                nc.vector.scalar_tensor_tensor(per_batch(zT[:, :]), per_batch(bank[:, :]), biasT[:, bias:bias + 1],
                                               ada(r, s.t), ALU.add, ALU.mult).then_inc(done, 1)

            def add_branch(s, ps_done, done):
                dve.wait_ge(ps_done, s.t + 1 + FREE)
                nc.vector.tensor_tensor(tokens(s.t), ps_m[0][:, :], tokens(s.t), ALU.add).then_inc(done, 1)

            for done in (x2_ready, z_ready, z2_ready, y_ready):
                dve.sem_inc(done, FREE)
            def stats_of(t):
                for j in range(SB):
                    group_stats(t, j)

            dve.wait_ge(x_in[0], 16)
            stats_of(0)
            dve.wait_ge(bn_done, SB)
            combine(0, 0, SB)
            dve.wait_ge(id_ready, 1)
            nc.vector.tensor_reduce(kmask[:, :], ident[:, :].rearrange("p (g h d) -> p h g d", g=HQ, h=Q4),
                                    axis=AX.XY, op=ALU.add).then_inc(kmask_ready, 1)
            dve.wait_ge(setupT_ready, 1)
            nc.vector.tensor_copy(condT[:, :], ps_m[1][:, 0:P]).then_inc(setupT_copied, 1)
            dve.wait_ge(setupT_ready, 2)
            nc.vector.tensor_copy(biasT[:, 0:NB0], ps_p[0][:, 0:NB0]).then_inc(setupT_copied, 1)
            dve.wait_ge(setupT_copied, 2)
            dve.wait_ge(kmask_ready, 1)
            nc.vector.tensor_scalar(kbias[:, :], kmask[:, :], biasT[:, K_B:K_B + 1], None, ALU.mult).then_inc(
                kbias_ready, 1)

            def take_condition(count, r, bank):
                dve.wait_ge(ada_ps, count)
                nc.vector.tensor_scalar(adaT[:, r, :], bank[:, :B], biasT[:, ADA_B + r:ADA_B + r + 1],
                                        1.0 if r in (SCALE1, SCALE2) else 0.0, ALU.add, ALU.add).then_inc(ada_ready, 1)

            take_condition(1, SCALE1, ps_o[0])
            take_condition(2, SHIFT1, ps_o[1])
            dve.wait_ge(ada_ready, 2)
            scale_h(Step(0, 0), 0, True)
            dve.memset(kexp[0][:, 0:H // 2, :], 0.0).then_inc(kexp_zero[0], 1)
            dve.wait_ge(x_in[1], 16)
            stats_of(1)
            dve.wait_ge(bn_done, 2 * SB)
            dve.wait_ge(rstd_ready, 1)
            combine(0, SB, 2 * SB)
            take_condition(3, GATE1, ps_s[0])
            take_condition(4, SHIFT2, ps_s[1])
            take_condition(5, SCALE2, ps_o[0])
            take_condition(6, GATE2, ps_o[1])
            dve.wait_ge(setupT_ready, 3)
            nc.vector.tensor_copy(biasT[:, NB0:NB0 + NB1], ps_p[1][:, 0:NB1]).then_inc(setupT_copied, 1)
            v_blocks(Step(0, 0), True)
            for p in range(2):
                dve.memset(kexp[1][:, p * H // 2:(p + 1) * H // 2, :], 0.0).then_inc(kexp_zero[1], 1)

            def attend(s, first, final):
                for j in range(SB):
                    n = s.t * SB + j
                    less_max(n, j, first and j < 2)
                    if j == 0 and not final:
                        scale_h(s.plus(1), 0, first)
                    if j == 3 and not first:
                        gate(s.plus(-1), GATE1, O_B, ps_m[1], wo_ps, zT_ps, z_ready)
                    if not (first and j < 2):
                        normalize_heads(s if j > 1 else s.plus(-1), (j - 2) % SB, n - 2, first)
                    if j == 2 and not final:
                        v_blocks(s.plus(1))
                    if j == 3 and not first:
                        add_branch(s.plus(-1), zT_ps, x2_ready)
                        dve.wait_ge(x2_ready, s.t + FREE)
                        stats_of(s.plus(-1).t)
                    if first:
                        for t in ((2,), (3, 4), (5, 6), (7,))[j]:
                            dve.wait_ge(x_in[t], 16)
                            stats_of(t)
                        if j == 0:
                            dve.wait_ge(bn_done, 3 * SB)
                            dve.wait_ge(rstd_ready, 2)
                            combine(0, 2 * SB, 3 * SB)
                        if j == 3:
                            dve.wait_ge(bn_done, GROUPS)
                            dve.wait_ge(rstd_ready, 3)
                            combine(0, 3 * SB, GROUPS)
                    if final and j == 0:
                        dve.wait_ge(bn_done, GROUPS + (NS - 2) * SB)
                        dve.wait_ge(rstd_ready, 4)
                        combine(1, 0, (NS - 2) * SB)

            both_phases_loop(dve, attend)
            last_s = Step(NS // 2 - 1, 1)
            normalize_heads(last_s, SB - 2, GROUPS - 2, False)
            scale_h(Step(0, 0), 1, True)
            normalize_heads(last_s, SB - 1, GROUPS - 1, False)
            gate(last_s, GATE1, O_B, ps_m[1], wo_ps, zT_ps, z_ready)
            scale_h(Step(0, 1), 1, True)
            add_branch(last_s, zT_ps, x2_ready)
            dve.wait_ge(x2_ready, NS + FREE)
            stats_of(last_s.t)
            dve.wait_ge(bn_done, 2 * GROUPS)
            dve.wait_ge(rstd_ready, 5)
            combine(1, (NS - 2) * SB, GROUPS)

            def feed(s, first, final):
                if not first:
                    gate(s.plus(-1), GATE2, F2_B, ps_o[0], w2_ps, z2T_ps, z2_ready)
                    add_branch(s.plus(-1), z2T_ps, y_ready)
                    if not final:
                        scale_h(s.plus(1), 1)

            both_phases_loop(dve, feed)
            gate(last_s, GATE2, F2_B, ps_o[0], w2_ps, z2T_ps, z2_ready)
            add_branch(last_s, z2T_ps, y_ready)


_INS = ['x', 'cond_1024', 'L0_cond_W_ada', 'L0_cond_b_ada', 'L0_cond_Wq', 'L0_cond_bq', 'L0_cond_Wk', 'L0_cond_bk',
        'L0_cond_Wv', 'L0_cond_bv', 'L0_cond_Wo', 'L0_cond_bo', 'L0_cond_W1', 'L0_cond_b1', 'L0_cond_W2',
        'L0_cond_b2']


def kernel(**inputs):
    import numpy as _np
    import concourse.bacc as _bacc
    from concourse import mybir as _mybir
    from concourse.bass_utils import run_bass_kernel_spmd as _run

    nc = _bacc.Bacc("TRN2", target_bir_lowering=False, num_devices=1)
    arrays, args = {}, []
    for name in _INS:
        a = _np.ascontiguousarray(inputs[name])
        arrays[f"in_{name}_dram"] = a
        args.append(nc.dram_tensor(f"in_{name}_dram", a.shape, _mybir.dt.from_np(a.dtype), kind="ExternalInput").ap())
    shape = inputs["x"].shape
    args.append(nc.dram_tensor("out_0_dram", shape, _mybir.dt.float32, kind="ExternalOutput").ap())
    dit_block(nc, *args)
    r = _run(nc, [arrays], core_ids=[0])
    return r.results[0]["out_0_dram"]
```

```python
from contextlib import ExitStack

import concourse.bass as bass
from concourse import mybir

F32 = mybir.dt.float32
F32R = mybir.dt.float32r
ALU = mybir.AluOpType
ACT = mybir.ActivationFunctionType
AX = mybir.AxisListType


class Step:

    def __init__(self, pair, parity):
        self.pair, self.parity = pair, parity
        self.t = pair * 2 + parity

    def plus(self, d):
        parity = (self.parity + d) % 2
        return Step(self.pair + (self.parity + d - parity) // 2, parity)


def dit_block(nc, x, cond, W_ada, b_ada, Wq, bq, Wk, bk, Wv, bv, Wo, bo, W1, b1, W2, b2, out):
    B, N, D = x.shape
    P = 128
    HD = 8
    H = D // HD
    Q4 = 4
    HQ = H // Q4
    FF = W1.shape[1]
    FC = FF // P
    GROUPS = B // Q4
    SB = 4
    T = SB * P
    NS = GROUPS // SB
    BS = SB * Q4
    VW = HD + 1
    EPS = 1e-05
    ZERO_DVE, ZERO_POOL = 4, 12
    SCALE = float(1.0 / (HD ** 0.5))
    K0_PIECES = (slice(0, P), slice(P, T))
    KINC = 16 * HQ
    FREE = 1
    assert N == 32 and D == P and B % (Q4 * SB) == 0 and NS % 2 == 0

    with ExitStack() as ctx:
        def sb(name, shape, dtype=F32):
            return ctx.enter_context(nc.sbuf_tensor(name, shape, dtype))

        def pb(name):
            return ctx.enter_context(nc.psum_tensor(name, [P, T], F32))

        def sem(name):
            return ctx.enter_context(nc.semaphore(name))

        x_sb = sb("x_sb", [P, NS * T])
        wada_sb = sb("wada_sb", [P, 6 * D])
        cond_sb = sb("cond_sb", [B, D])
        condT = sb("condT", [D, B])
        wq_sb, wk_sb, wv_in, wv_sb, wo_sb = (sb(n, [P, D]) for n in ("wq_sb", "wk_sb", "wv_in", "wv_sb", "wo_sb"))
        w1_sb = sb("w1_sb", [P, FF])
        w2_sb = sb("w2_sb", [P, FC * D])
        bias_rows = [sb(f"bias_rows{i}", [P, P]) for i in range(2)]
        NB0, NB1 = 9, 2 + FC
        biasT = sb("biasT", [P, NB0 + NB1])
        ADA_B, Q_B, K_B, V_B, O_B, F2_B, F1_B = 0, 6, 7, 8, NB0, NB0 + 1, NB0 + 2
        kmask = sb("kmask", [P, Q4])
        vmask = sb("vmask", [P, Q4])
        kbias = sb("kbias", [P, Q4])
        adaT = sb("adaT", [D, 6, B])
        ident = sb("ident", [P, P])
        minus_half = sb("minus_half", [P, GROUPS])
        zeros = sb("zeros", [P, T])
        bn = sb("bn", [P, GROUPS, 6])
        mean, rstd = sb("mean", [P, GROUPS]), sb("rstd", [P, GROUPS])
        ln_dif, ln_m2, ln_sq, ln_var = (sb(n, [P, GROUPS]) for n in ("ln_dif", "ln_m2", "ln_sq", "ln_var"))
        xn = [sb(f"xn{i}", [P, T]) for i in range(2)]
        hT = [sb(f"hT{i}", [D, T]) for i in range(2)]
        qT = [sb(f"qT{i}", [P, T]) for i in range(2)]
        kTm = sb("kTm", [P, Q4, T])
        vT = sb("vT", [P, T])
        vx = sb("vx", [P, T])
        kexp = [sb(f"kexp{i}", [P, H, T]) for i in range(2)]
        vexp = [sb(f"vexp{i}", [P, BS, Q4, HQ, VW]) for i in range(2)]
        smax = [sb(f"smax{i}", [P, H]) for i in range(2)]
        sdif = [sb(f"sdif{i}", [P, H * N]) for i in range(2)]
        prob = [sb(f"prob{i}", [P, H * N]) for i in range(2)]
        probT = [sb(f"probT{i}", [P, H * N]) for i in range(2)]
        rsum = [sb(f"rsum{i}", [P, H]) for i in range(2)]
        attn = [sb(f"attn{i}", [P, SB, D]) for i in range(2)]
        attnT = sb("attnT", [P, T])
        zT = sb("zT", [D, T])
        hid = sb("hid", [P, FC, T])
        h_hi, h_lo = ([sb(f"{n}{i}", [D, T], F32R) for i in range(2)] for n in ("h_hi", "h_lo"))
        wk_hi, wk_lo, wq_hi, wq_lo, wv_hi, wv_lo = (sb(n, [P, D], F32R) for n in (
            "wk_hi", "wk_lo", "wq_hi", "wq_lo", "wv_hi", "wv_lo"))
        w1_hi, w1_lo = (sb(n, [P, FF], F32R) for n in ("w1_hi", "w1_lo"))
        w2_hi, w2_lo = (sb(n, [P, FC * D], F32R) for n in ("w2_hi", "w2_lo"))
        hid_hi, hid_lo = (sb(n, [P, FC, T], F32R) for n in ("hid_hi", "hid_lo"))

        ps_s = [pb("ps_s0"), pb("ps_s1")]
        ps_p, ps_o = pb("ps_p"), pb("ps_o")
        ps_x, ps_k, ps_q = pb("ps_x"), pb("ps_k"), pb("ps_q")
        ps_b = pb("ps_b")
        ps_ff = [ps_k, ps_q, ps_s[0], ps_s[1]]
        ps_w = [ps_o, ps_p]

        x_in = [sem(f"x_in{t}") for t in range(NS)]
        (w_ada_in, w_qkv_in, w_late_in) = map(sem, ("w_ada_in", "w_qkv_in", "w_late_in"))
        rows_in = [sem(f"rows_in{i}") for i in range(2)]
        (rows_zero, id_zero, id_ready, consts_ready, zeros_ready, vmask_ready, vexp_ones, wv_ready) = map(sem, (
            "rows_zero", "id_zero", "id_ready", "consts_ready", "zeros_ready", "vmask_ready", "vexp_ones", "wv_ready"))
        kexp_zero = [sem(f"kexp_zero{i}") for i in range(2)]
        (setupT_ready, setupT_copied, ada_ps, ada_ready, kmask_ready, kbias_ready, table_loaded) = map(sem, (
            "setupT_ready", "setupT_copied", "ada_ps", "ada_ready", "kmask_ready", "kbias_ready", "table_loaded"))
        (xn0_ready, h0_ready, k0_dve, k0_act) = map(sem, ("xn0_ready", "h0_ready", "k0_dve", "k0_act"))
        (bn_done, ln_step, ln_ready, rstd_ready, xn_sub, xn_ready) = map(sem, (
            "bn_done", "ln_step", "ln_ready", "rstd_ready", "xn_sub", "xn_ready"))
        (whi_ready, wlo_ready, ff_wlo_ready, hhi_ready, hlo_ready, hid_lo_ready) = map(sem, (
            "whi_ready", "wlo_ready", "ff_wlo_ready", "hhi_ready", "hlo_ready", "hid_lo_ready"))
        (xnT_ps, h_scaled, h_ready) = map(sem, ("xnT_ps", "h_scaled", "h_ready"))
        (q_ps, k_ps, v_ps, q_ready, k_ready, v_ready, vx_ready, vexp_ready) = map(sem, (
            "q_ps", "k_ps", "v_ps", "q_ready", "k_ready", "v_ready", "vx_ready", "vexp_ready"))
        kexp_in = [sem(f"kexp_in{i}") for i in range(2)]
        (s_ps, max_ready, dif_ready, prob_ready, probT_ps, probT_ready, o_ps, rsum_ready, attn_ready) = map(sem, (
            "s_ps", "max_ready", "dif_ready", "prob_ready", "probT_ps", "probT_ready", "o_ps", "rsum_ready",
            "attn_ready"))
        (attnT_ps, attnT_ready, wo_ps, z_ready, zT_ps, x2_ready) = map(sem, (
            "attnT_ps", "attnT_ready", "wo_ps", "z_ready", "zT_ps", "x2_ready"))
        (ff_ps, hid_ready, w2_ps, z2_ready, z2T_ps, y_ready, y_out) = map(sem, (
            "ff_ps", "hid_ready", "w2_ps", "z2_ready", "z2T_ps", "y_ready", "y_out"))

        def tokens(t):
            return x_sb[:, bass.ds(t * T, T)]

        def ada(r, t):
            return adaT[:, r, bass.ds(t * BS, BS)].unsqueeze(2).to_broadcast([D, BS, N])

        def per_batch(ap):
            return ap.rearrange("p (b q) -> p b q", q=N)

        def along_features(stat):
            return stat.unsqueeze(2).to_broadcast([P, SB, D])

        SHIFT1, SCALE1, GATE1, SHIFT2, SCALE2, GATE2 = range(6)
        block = ctx.enter_context(nc.Block())

        def superblocks(eng, body):
            body(Step(0, 0), 0, NS - 1)
            body(Step(0, 1), 1, NS - 2)
            with eng.Fori(1, NS // 2 - 1) as i:
                body(Step(i, 0), 2, 2)
                body(Step(i, 1), 2, 2)
            body(Step(NS // 2 - 1, 0), NS - 2, 1)
            body(Step(NS // 2 - 1, 1), NS - 1, 0)

        def kexp_count(s):
            return (s.pair + s.parity) * KINC

        def front_slot(before, after):
            return 3 if not before or after == 1 else 1 if after else None

        def ahead(s, after):
            return (s.plus(2), 0) if after >= 2 else (Step(0, s.parity), 1)

        @block.sync
        def _(sp):
            def load_x(t):
                sp.dma_start(x_sb[:, t * T:(t + 1) * T].rearrange("p (g d) -> p g d", g=SB),
                             x[t * BS:(t + 1) * BS].rearrange("(g b) q d -> (b q) g d", g=SB)).then_inc(x_in[t], 16)

            def load_row(i, src, r, n):
                sp.dma_start(bias_rows[i][r:r + n, :], src.rearrange("(r p) -> r p", p=P)).then_inc(rows_in[i], 16)

            load_x(0)
            sp.wait_ge(rows_zero, 2)
            load_row(0, b_ada, ADA_B, 6)
            load_row(0, bk, K_B, 1)
            load_row(0, bq, Q_B, 1)
            sp.dma_start(bias_rows[0][V_B:V_B + 1, :].rearrange("o (h g d) -> o h g d", h=Q4, g=HQ),
                         bv.rearrange("(o g h d) -> o h g d", o=1, g=HQ, h=Q4)).then_inc(rows_in[0], 16)
            load_x(1)
            load_x(2)
            load_row(1, bo, 0, 1)
            load_row(1, b2, 1, 1)
            load_row(1, b1, 2, FC)
            load_x(3)
            sp.dma_start(wo_sb[:, :], Wo).then_inc(w_late_in, 16)
            sp.dma_start(w1_sb[:, :], W1).then_inc(w_late_in, 16)
            sp.dma_start(w2_sb[:, :].rearrange("p (c d) -> p c d", c=FC),
                         W2.rearrange("(c p) d -> p c d", p=P)).then_inc(w_late_in, 16)
            for t in range(4, NS):
                load_x(t)

            def expand_k(s, early=False):
                sp.wait_ge(k_ready, s.t + 1)
                if not early:
                    sp.wait_ge(s_ps, s.t * SB - SB)
                for g in range(HQ):
                    rows = slice(g * Q4 * HD, (g + 1) * Q4 * HD)
                    sp.dma_start(kexp[s.parity][rows, g * Q4:(g + 1) * Q4, :],
                                 kTm[rows, :, :]).then_inc(kexp_in[s.parity], 16)

            sp.wait_ge(kexp_zero[1], 2)
            expand_k(Step(0, 1), True)
            with sp.Fori(1, NS // 2) as i:
                expand_k(Step(i, 0))
                expand_k(Step(i, 1))
            with sp.Fori(0, NS) as t:
                sp.wait_ge(y_ready, t + 1 + FREE)
                sp.dma_start(out[bass.ds(t * BS, BS)].rearrange("(g b) q d -> (b q) g d", g=SB),
                             tokens(t).rearrange("p (g d) -> p g d", g=SB)).then_inc(y_out, 16)
            sp.wait_ge(y_out, 16 * NS)

        @block.gpsimd
        def _(pool):
            for i in range(2):
                pool.memset(bias_rows[i][:, :], 0.0).then_inc(rows_zero, 1)
            pool.memset(ident[:, :], 0.0).then_inc(id_zero, 1)
            pool.memset(zeros[:, :], 0.0).then_inc(zeros_ready, 1)
            pool.memset(minus_half[:, :], -0.5).then_inc(consts_ready, 1)
            pool.wait_ge(id_zero, 1)
            pool.affine_select(out=ident[:, :], in_=ident[:, :], compare_op=ALU.not_equal, fill=1.0, base=0,
                               pattern=[[-1, P]], channel_multiplier=1).then_inc(id_ready, 1)
            pool.memset(kexp[0][:, ZERO_DVE:ZERO_POOL, :], 0.0).then_inc(kexp_zero[0], 1)

            def rstd_of(t0, t1, vars_done, count):
                c = slice(t0 * SB, t1 * SB)
                pool.wait_ge(ln_ready, vars_done)
                pool.tensor_tensor(rstd[:, c], ln_var[:, c], minus_half[:, c], ALU.pow).then_inc(rstd_ready, 1)
                pool.wait_ge(rstd_ready, count)

            def normalize(s, ln, unused=False):
                n = ln * NS
                mean_s, rstd_s = mean[:, bass.ds(s.t * SB, SB)], rstd[:, bass.ds(s.t * SB, SB)]
                if not unused:
                    pool.wait_ge(xnT_ps, s.t - 1 + n)
                pool.wait_ge(consts_ready, 1)
                x3 = tokens(s.t).rearrange("p (g d) -> p g d", g=SB)
                xn3 = xn[s.parity][:, :].rearrange("p (g d) -> p g d", g=SB)
                nc.gpsimd.tensor_tensor(xn3, x3, along_features(mean_s), ALU.subtract).then_inc(xn_sub, 1)
                pool.wait_ge(xn_sub, s.t + 1 + n)
                pool.wait_ge(consts_ready, 1)
                nc.gpsimd.tensor_tensor(xn3, xn3, along_features(rstd_s), ALU.mult).then_inc(xn_ready, 1)

            def shift(s, ln):
                n = ln * NS
                pool.wait_ge(h_scaled, s.t + 1 + n)
                pool.wait_ge(consts_ready, 1)
                h = per_batch(hT[s.parity][:, :])
                nc.gpsimd.tensor_tensor(h, h, ada(SHIFT2 if ln else SHIFT1, s.t), ALU.add).then_inc(h_ready, 1)

            def low_of_h(s, ln):
                pool.wait_ge(hhi_ready, s.t + 1 + ln * NS)
                nc.gpsimd.tensor_tensor(h_lo[s.parity][:, :], hT[s.parity][:, :], h_hi[s.parity][:, :],
                                        ALU.subtract).then_inc(hlo_ready, 1)

            def place_v(s, early=False):
                pool.wait_ge(vx_ready, s.t + 1)
                if not early:
                    pool.wait_ge(o_ps, s.t * SB - SB)
                pool.wait_ge(vmask_ready, 1)
                for h4 in range(Q4):
                    nc.gpsimd.tensor_tensor(vexp[s.parity][:, :, h4, :, 0:HD],
                                            vx[:, :].rearrange("k (b g d) -> k b g d", b=BS, g=HQ),
                                            vmask[:, h4:h4 + 1].unsqueeze(2).unsqueeze(3).to_broadcast([P, BS, HQ, HD]),
                                            ALU.mult).then_inc(vexp_ready, 1)

            pool.wait_ge(consts_ready, 1)
            rstd_of(0, 1, 1, 1)
            for done in (xn_sub, xn_ready, h_ready, hlo_ready):
                pool.sem_inc(done, 1)
            pool.wait_ge(w_qkv_in, 48)
            pool.tensor_copy(wv_sb[:, :].rearrange("p (h g d) -> p h g d", h=Q4, g=HQ),
                             wv_in[:, :].rearrange("p (g h d) -> p h g d", h=Q4, g=HQ)).then_inc(wv_ready, 1)
            pool.memset(kexp[1][:, 0:H // 2, :], 0.0).then_inc(kexp_zero[1], 1)
            pool.wait_ge(whi_ready, 3)
            for lo, whole, hi in ((wk_lo, wk_sb, wk_hi), (wq_lo, wq_sb, wq_hi), (wv_lo, wv_sb, wv_hi)):
                nc.gpsimd.tensor_tensor(lo[:, :], whole[:, :], hi[:, :], ALU.subtract).then_inc(wlo_ready, 1)
            rstd_of(1, 2, 2, 2)
            normalize(Step(0, 1), 0, True)
            shift(Step(0, 1), 0)
            low_of_h(Step(0, 1), 0)
            place_v(Step(0, 0), True)
            rstd_of(2, 4, 3, 3)

            def attend(s, before, after):
                u, ln = ahead(s, after)
                if after > 1:
                    normalize(u, ln)
                if before:
                    place_v(s, before < 2)
                if before == 1:
                    rstd_of(4, NS, 4, 4)
                if after == 1:
                    rstd_of(0, 2, 5, 5)
                if after < 2:
                    normalize(u, ln)
                if after:
                    shift(u, ln)
                    low_of_h(u, ln)

            superblocks(pool, attend)

            rstd_of(2, 5, 6, 6)
            shift(Step(0, 1), 1)
            normalize(Step(1, 0), 1)
            low_of_h(Step(0, 1), 1)
            normalize(Step(1, 1), 1)
            shift(Step(1, 0), 1)
            low_of_h(Step(1, 0), 1)
            normalize(Step(2, 0), 1)
            shift(Step(1, 1), 1)
            low_of_h(Step(1, 1), 1)
            rstd_of(5, NS, 7, 7)
            shift(Step(2, 0), 1)
            normalize(Step(2, 1), 1)
            low_of_h(Step(2, 0), 1)
            for t in range(5, NS):
                s = Step(t // 2, t % 2)
                if t < NS - 1:
                    normalize(s.plus(1), 1)
                shift(s, 1)
                low_of_h(s, 1)

        @block.tensor
        def _(pe):
            for done in (attnT_ps, wo_ps, zT_ps, z2T_ps):
                pe.sem_inc(done, FREE)

            def xn_transposes(s, ln, waited=False):
                if not waited:
                    pe.wait_ge(xn_ready, s.t + 1 + ln * NS)
                for j in range(SB):
                    last = nc.tensor.transpose(ps_x[:, j * P:(j + 1) * P], xn[s.parity][:, j * P:(j + 1) * P],
                                               ident[:, :])
                last.then_inc(xnT_ps, 1)

            def project0(w, bank, done):
                nc.tensor.matmul(bank[:, :], w[:, :], hT[0][:, :], start=True, stop=True).then_inc(done, 1)

            def project(s, weights, bank, done):
                split_product(bank, weights, slice(0, D), s, done)

            def split_product(bank, weights, own, s, done):
                w_hi, w_lo = weights
                hi, lo = h_hi[s.parity][:, :], h_lo[s.parity][:, :]
                nc.tensor.matmul(bank[:, :], w_lo[:, own], hi, start=True, stop=False)
                nc.tensor.matmul(bank[:, :], w_hi[:, own], lo, start=False, stop=False)
                nc.tensor.matmul(bank[:, :], w_hi[:, own], hi, start=False, stop=True).then_inc(done, 1)

            def scores(s, j):
                for b in range(Q4):
                    q = slice(j * P + b * N, j * P + (b + 1) * N)
                    last = nc.tensor.matmul(ps_s[j % 2][b * N:(b + 1) * N, :], qT[s.parity][:, q],
                                            kexp[s.parity][:, :, q], start=True, stop=True)
                last.then_inc(s_ps, 1)

            def prob_transposes(j):
                for g in range(HQ):
                    c = slice(g * P, (g + 1) * P)
                    last = nc.tensor.transpose(ps_p[:, c], prob[j % 2][:, c], ident[:, :])
                last.then_inc(probT_ps, 1)

            def values(s, j):
                for b in range(Q4):
                    for g in range(HQ):
                        o = g * Q4 * VW
                        last = nc.tensor.matmul(ps_o[b * N:(b + 1) * N, o:o + Q4 * VW],
                                                probT[j % 2][:, g * P + b * N:g * P + (b + 1) * N],
                                                vexp[s.parity][:, j * Q4 + b, :, g, :], start=True, stop=True)
                last.then_inc(o_ps, 1)

            pe.wait_ge(id_ready, 1)
            pe.wait_ge(w_ada_in, 32)
            nc.tensor.transpose(ps_b[:, 0:P], cond_sb[:, :], ident[:, :]).then_inc(setupT_ready, 1)
            pe.wait_ge(rows_in[0], 16 * 4)
            nc.tensor.transpose(ps_p[:, 0:P], bias_rows[0][:, :], ident[:, :]).then_inc(setupT_ready, 1)
            pe.wait_ge(setupT_copied, 1)

            def condition(r, bank):
                nc.tensor.matmul(bank[:, :B], wada_sb[:, r * D:(r + 1) * D], condT[:, :],
                                 start=True, stop=True).then_inc(ada_ps, 1)

            condition(SCALE1, ps_o)
            condition(SHIFT1, ps_q)
            pe.wait_ge(xn0_ready, 1)
            xn_transposes(Step(0, 0), 0, True)
            condition(GATE1, ps_s[0])
            condition(SHIFT2, ps_s[1])
            pe.wait_ge(setupT_copied, 2)
            condition(SCALE2, ps_p)
            condition(GATE2, ps_b)
            pe.wait_ge(h0_ready, 1)
            pe.wait_ge(w_qkv_in, 48)
            project0(wk_sb, ps_k, k_ps)
            project0(wq_sb, ps_q, q_ps)
            pe.wait_ge(ada_ready, 6)
            pe.wait_ge(rows_in[1], 16 * 3)
            nc.tensor.transpose(ps_p[:, 0:P], bias_rows[1][:, :], ident[:, :]).then_inc(setupT_ready, 1)
            pe.wait_ge(wv_ready, 1)
            pe.wait_ge(q_ready, 1)
            project0(wv_sb, ps_q, v_ps)
            xn_transposes(Step(0, 1), 0)

            def up(s, c, first=False):
                if c == 0:
                    pe.wait_ge(hlo_ready, s.t + 1 + NS)
                if not first:
                    pe.wait_ge(hid_ready, s.t * FC - FC + c + 1)
                split_product(ps_ff[c], (w1_hi, w1_lo), slice(c * P, (c + 1) * P), s, ff_ps)

            def attend(s, before, after):
                def transpose_ahead():
                    pe.wait_ge(h_scaled, s.t + 2)
                    xn_transposes(*ahead(s, after))

                for j in range(SB):
                    n = s.t * SB + j
                    if j == 0:
                        pe.wait_ge(q_ready, s.t + 1)
                        if before:
                            pe.wait_ge(kexp_in[s.parity], kexp_count(s))
                    if not before and j < 2:
                        pe.wait_ge(k0_dve, j + 1)
                        pe.wait_ge(k0_act, j + 1)
                    if before or j > 1:
                        pe.wait_ge(dif_ready, n - 1)
                    scores(s, j)
                    if j == (0 if before > 1 else 1) and after:
                        if not before:
                            pe.wait_ge(wlo_ready, 3)
                            pe.wait_ge(k0_dve, 2)
                        pe.wait_ge(hlo_ready, s.t + 2)
                        pe.wait_ge(k_ready, s.t + 1)
                        project(s.plus(1), (wk_hi, wk_lo), ps_k, k_ps)
                    if j == 1 and after:
                        pe.wait_ge(v_ready, s.t + 1)
                        project(s.plus(1), (wq_hi, wq_lo), ps_q, q_ps)
                    if j == 1 and not after:
                        pe.wait_ge(ff_wlo_ready, 2)
                        pe.wait_ge(k_ready, NS)
                        up(Step(0, 0), 0, True)
                    if j == 3 and not after:
                        pe.wait_ge(v_ready, NS)
                        up(Step(0, 0), 1, True)
                    if j == 2 and before:
                        attn_transposes(s.plus(-1), before > 1)
                    if j == 3 and after:
                        pe.wait_ge(q_ready, s.t + 2)
                        project(s.plus(1), (wv_hi, wv_lo), ps_q, v_ps)
                    if not before and j == front_slot(before, after):
                        transpose_ahead()
                    if not before and j == 1:
                        pe.wait_ge(setupT_copied, 3)
                    if before or j > 0:
                        pe.wait_ge(prob_ready, n)
                        if before or j > 1:
                            pe.wait_ge(probT_ready, n - 1)
                        prob_transposes((j - 1) % SB)
                    if before or j > 1:
                        own = s if j > 1 else s.plus(-1)
                        pe.wait_ge(probT_ready, n - 1)
                        pe.wait_ge(vexp_ready, own.t * Q4 + Q4)
                        if not before and j == 2:
                            pe.wait_ge(vexp_ones, 2)
                        if before or j > 2:
                            pe.wait_ge(attn_ready, n - 2)
                        values(own, (j - 2) % SB)
                    if j == 0 and before > 1:
                        branch_transposes(s.plus(-2))
                    if before and j == front_slot(before, after):
                        transpose_ahead()
                    if j == 3 and before:
                        out_project(s.plus(-1))

            def attn_transposes(s, used=True):
                pe.wait_ge(attn_ready, s.t * SB + SB)
                if used:
                    pe.wait_ge(x2_ready, s.t + FREE)
                for j in range(SB):
                    last = nc.tensor.transpose(ps_b[:, j * P:(j + 1) * P], attn[s.parity][:, j, :], ident[:, :])
                last.then_inc(attnT_ps, 1)

            def out_project(s):
                pe.wait_ge(w_late_in, 48)
                pe.wait_ge(attnT_ready, s.t + 1)
                nc.tensor.matmul(ps_b[:, :], wo_sb[:, :], attnT[:, :], start=True, stop=True).then_inc(wo_ps, 1)

            def branch_transposes(s):
                pe.wait_ge(z_ready, s.t + 1 + FREE)
                for j in range(SB):
                    last = nc.tensor.transpose(ps_b[:, j * P:(j + 1) * P], zT[:, j * P:(j + 1) * P], ident[:, :])
                last.then_inc(zT_ps, 1)

            superblocks(pe, attend)

            def down(s, c, first=False):
                pe.wait_ge(hid_lo_ready, s.t * FC + c + 1)
                if c == 0 and not first:
                    pe.wait_ge(z2_ready, s.t - 1 + FREE)
                own = slice(c * D, (c + 1) * D)
                bank = ps_w[s.parity]
                nc.tensor.matmul(bank[:, :], w2_lo[:, own], hid_hi[:, c, :], start=(c == 0), stop=False)
                nc.tensor.matmul(bank[:, :], w2_hi[:, own], hid_lo[:, c, :], start=False, stop=False)
                nc.tensor.matmul(bank[:, :], w2_hi[:, own], hid_hi[:, c, :], start=False,
                                 stop=(c == FC - 1)).then_inc(w2_ps, 1)

            last_s = Step(NS // 2 - 1, 1)
            s0 = Step(0, 0)
            pe.wait_ge(prob_ready, GROUPS)
            pe.wait_ge(probT_ready, GROUPS - 1)
            prob_transposes(SB - 1)
            pe.wait_ge(attn_ready, GROUPS - 2)
            values(last_s, SB - 2)
            pe.wait_ge(dif_ready, GROUPS)
            up(s0, 2, True)
            pe.wait_ge(h_scaled, NS + 1)
            xn_transposes(s0.plus(1), 1)
            branch_transposes(last_s.plus(-1))
            pe.wait_ge(probT_ready, GROUPS)
            pe.wait_ge(attn_ready, GROUPS - 1)
            values(last_s, SB - 1)
            up(s0, 3, True)
            attn_transposes(last_s)
            down(s0, 0, True)
            out_project(last_s)
            down(s0, 1)
            branch_transposes(last_s)

            def branch2_transposes(s):
                pe.wait_ge(z2_ready, s.t + 1 + FREE)
                pe.wait_ge(x2_ready, NS + FREE)
                pe.wait_ge(y_ready, s.t + FREE)
                for j in range(SB):
                    last = nc.tensor.transpose(ps_b[:, j * P:(j + 1) * P], zT[:, j * P:(j + 1) * P], ident[:, :])
                last.then_inc(z2T_ps, 1)

            def feed(s, before, after):
                for c in range(FC):
                    if before:
                        up(s, c)
                    if before and c < 2:
                        down(s.plus(-1), c + 2)
                    if before and c == 3:
                        branch2_transposes(s.plus(-1))
                    if before and c >= 2:
                        down(s, c - 2)
                if after > 1:
                    pe.wait_ge(h_scaled, s.t + 2 + NS)
                    xn_transposes(s.plus(2), 1)

            superblocks(pe, feed)
            down(last_s, 2)
            down(last_s, 3)
            branch2_transposes(last_s)

        @block.scalar
        def _(act):
            act.dma_start(wada_sb[:, :], W_ada).then_inc(w_ada_in, 16)
            act.dma_start(cond_sb[:, :], cond).then_inc(w_ada_in, 16)
            act.wait_ge(consts_ready, 1)
            nc.scalar.activation(prob[0][:, 0:1], minus_half[:, 0:1], ACT.Exp).then_inc(table_loaded, 1)
            for dst, src in ((wk_sb, Wk), (wq_sb, Wq), (wv_in, Wv)):
                act.dma_start(dst[:, :], src).then_inc(w_qkv_in, 16)

            def with_bias(dst, bank, r, done):
                nc.scalar.activation(dst, bank[:, :], ACT.Identity, bias=biasT[:, r:r + 1]).then_inc(done, 1)

            def take_k(s, h4, early=False):
                act.wait_ge(k_ps, s.t + 1)
                if h4 == 0 and not early:
                    act.wait_ge(kexp_in[1 - s.parity], kexp_count(s.plus(-1)))
                last = nc.scalar.activation(kTm[:, h4, :], ps_k[:, :], ACT.Identity,
                                            scale=kmask[:, h4:h4 + 1], bias=kbias[:, h4:h4 + 1])
                if h4 == Q4 - 1:
                    last.then_inc(k_ready, 1)

            def take_q(s, early=False):
                act.wait_ge(q_ps, s.t + 1)
                if not early:
                    act.wait_ge(s_ps, s.t * SB - SB)
                with_bias(qT[s.parity][:, :], ps_q, Q_B, q_ready)

            def take_v(s, early=False):
                act.wait_ge(v_ps, s.t + 1)
                if not early:
                    act.wait_ge(vx_ready, s.t)
                with_bias(vT[:, :], ps_q, V_B, v_ready)

            def exps(n, j, early=False):
                act.wait_ge(dif_ready, n + 1)
                if early:
                    act.wait_ge(table_loaded, 1)
                if not early:
                    act.wait_ge(probT_ps, n - 1)
                nc.scalar.activation(prob[j % 2][:, :], sdif[j % 2][:, :], ACT.Exp, scale=SCALE).then_inc(prob_ready, 1)

            def take_probT(n, j, early=False):
                act.wait_ge(probT_ps, n + 1)
                if not early:
                    act.wait_ge(o_ps, n - 1)
                nc.scalar.activation(probT[j % 2][:, :], ps_p[:, :], ACT.Copy).then_inc(probT_ready, 1)

            def gelu(s, c, first=False):
                act.wait_ge(ff_ps, s.t * FC + c + 1)
                if not first:
                    act.wait_ge(w2_ps, s.t * FC - FC + c + 1)
                bias = biasT[:, F1_B + c:F1_B + c + 1]
                nc.scalar.activation(hid_hi[:, c, :], ps_ff[c][:, :], ACT.Gelu, bias=bias)
                nc.scalar.activation(hid[:, c, :], ps_ff[c][:, :], ACT.Gelu, bias=bias).then_inc(hid_ready, 1)

            def take_attnT(t):
                act.wait_ge(attnT_ps, t + 1 + FREE)
                act.wait_ge(wo_ps, t + FREE)
                nc.scalar.activation(attnT[:, :], ps_b[:, :], ACT.Copy).then_inc(attnT_ready, 1)

            def high_of_h(s, ln, early=False, feeding=False):
                act.wait_ge(h_ready, s.t + 1 + ln * NS)
                if feeding:
                    act.wait_ge(ff_ps, s.t * FC - FC)
                elif not early:
                    act.wait_ge(v_ps, s.t - 1 + ln * NS)
                nc.scalar.activation(h_hi[s.parity][:, :], hT[s.parity][:, :], ACT.Copy).then_inc(hhi_ready, 1)

            act.wait_ge(zeros_ready, 1)
            nc.scalar.activation(kexp[0][:, ZERO_POOL:H, :], zeros[:, :].unsqueeze(1).to_broadcast(
                [P, H - ZERO_POOL, T]), ACT.Copy).then_inc(kexp_zero[0], 1)
            nc.scalar.activation(kexp[1][:, H // 2:H, :], zeros[:, :].unsqueeze(1).to_broadcast(
                [P, H // 2, T]), ACT.Copy).then_inc(kexp_zero[1], 1)

            def high_of_weights(parts):
                for hi, whole in parts:
                    nc.scalar.activation(hi[:, :], whole[:, :], ACT.Copy).then_inc(whi_ready, 1)

            act.sem_inc(hhi_ready, 1)
            act.wait_ge(w_qkv_in, 48)
            act.wait_ge(wv_ready, 1)
            high_of_weights(((wk_hi, wk_sb), (wq_hi, wq_sb), (wv_hi, wv_sb)))

            act.wait_ge(kbias_ready, 1)
            s0 = Step(0, 0)
            act.wait_ge(kexp_zero[0], 3)

            def place_k0(piece, g):
                act.wait_ge(k_ps, 1)
                rows, c = slice(g * P // HQ, (g + 1) * P // HQ), K0_PIECES[piece]
                for h4 in range(Q4):
                    last = nc.scalar.activation(kexp[0][rows, g * Q4 + h4, c], ps_k[rows, c], ACT.Identity,
                                                scale=kmask[rows, h4:h4 + 1], bias=kbias[rows, h4:h4 + 1])
                return last

            place_k0(0, 2)
            take_q(s0, True)
            place_k0(0, 3).then_inc(k0_act, 1)
            place_k0(1, 2)
            place_k0(1, 3).then_inc(k0_act, 1)
            act.sem_inc(k_ready, 1)
            high_of_h(Step(0, 1), 0, True)
            take_v(s0, True)
            def attend(s, before, after):
                for j in range(SB):
                    n = s.t * SB + j
                    if j == 0 and before > 1 and after:
                        take_k(s.plus(1), 0)
                    if j == 1 and after:
                        for h4 in range(2 if before > 1 else 0, Q4):
                            take_k(s.plus(1), h4)
                    if before or j > 0:
                        take_probT(n - 1, (j - 1) % SB, not before and j < 3)
                    if not before and j == 3:
                        high_of_h(*ahead(s, after))
                    exps(n, j, not before and j < 2)
                    if not before and j == 2:
                        act.wait_ge(w_late_in, 48)
                        high_of_weights(((w1_hi, w1_sb), (w2_hi, w2_sb)))
                    if j == 0 and before > 1 and after:
                        take_k(s.plus(1), 1)
                    if j == 1 and after:
                        take_q(s.plus(1), not before)
                    if j == 2 and before:
                        take_attnT(s.t - 1)
                    if j == 3 and after:
                        take_v(s.plus(1))
                    if j == (2 if front_slot(before, after) == 1 else 3) and before and after:
                        high_of_h(*ahead(s, after))

            superblocks(act, attend)
            take_probT(GROUPS - 1, SB - 1)
            for c in range(FC):
                if c == 2:
                    take_attnT(NS - 1)
                    high_of_h(s0.plus(1), 1)
                gelu(s0, c, True)

            def feed(s, before, after):
                for c in range(FC):
                    if before:
                        gelu(s, c)
                    if c == 1 and before and after:
                        high_of_h(s.plus(1), 1, feeding=True)

            superblocks(act, feed)

        @block.vector
        def _(dve):
            def group_stats(t, j):
                nc.vector.bn_stats(bn[:, bass.ds(t * SB + j, 1), :],
                                   x_sb[:, bass.ds(t * T + j * D, D)]).then_inc(bn_done, 1)

            def combine(c0, c1, k):
                c = slice(c0, c1)
                me, m2e, mo, m2o = (bn[:, c, i] for i in (1, 2, 4, 5))
                dif, m2, sq = ln_dif[:, c], ln_m2[:, c], ln_sq[:, c]
                nc.vector.tensor_tensor(mean[:, c], me, mo, ALU.add).then_inc(ln_step, 1)
                nc.vector.tensor_tensor(dif, me, mo, ALU.subtract).then_inc(ln_step, 1)
                nc.vector.tensor_tensor(m2, m2e, m2o, ALU.add).then_inc(ln_step, 1)
                dve.wait_ge(ln_step, k * 6 + 3)
                nc.vector.tensor_scalar(mean[:, c], mean[:, c], 0.5, None, ALU.mult).then_inc(ln_step, 1)
                nc.vector.scalar_tensor_tensor(sq, dif, 0.25, dif, ALU.mult, ALU.mult).then_inc(ln_step, 1)
                nc.vector.tensor_scalar(m2, m2, 1.0 / D, EPS, ALU.mult, ALU.add).then_inc(ln_step, 1)
                dve.wait_ge(ln_step, k * 6 + 6)
                nc.vector.tensor_tensor(ln_var[:, c], m2, sq, ALU.add).then_inc(ln_ready, 1)

            def scale_h(s, ln, early=False):
                n = ln * NS
                dve.wait_ge(xnT_ps, s.t + 1 + n)
                if not early:
                    dve.wait_ge(hlo_ready, s.t - 1 + n)
                nc.vector.tensor_tensor(per_batch(hT[s.parity][:, :]), per_batch(ps_x[:, :]),
                                        ada(SCALE2 if ln else SCALE1, s.t), ALU.mult).then_inc(h_scaled, 1)

            def v_blocks(s, early=False):
                dve.wait_ge(v_ready, s.t + 1)
                if not early:
                    dve.wait_ge(vexp_ready, s.t * Q4)
                nc.vector.transpose(vx[:, :], vT[:, :]).then_inc(vx_ready, 1)

            def less_max(n, j, early=False):
                heads = ps_s[j % 2][:, :].rearrange("p (h k) -> p h k", h=H)
                dve.wait_ge(s_ps, n + 1)
                if not early:
                    dve.wait_ge(dif_ready, n - 1)
                nc.vector.tensor_reduce(smax[j % 2][:, :], heads, axis=AX.X, op=ALU.max).then_inc(max_ready, 1)
                dve.wait_ge(max_ready, n + 1)
                if not early:
                    dve.wait_ge(prob_ready, n - 1)
                nc.vector.tensor_tensor(sdif[j % 2][:, :].rearrange("p (h k) -> p h k", h=H), heads,
                                        smax[j % 2][:, :].unsqueeze(2).to_broadcast([P, H, N]),
                                        ALU.subtract).then_inc(dif_ready, 1)

            def normalize_heads(s, j, n, early):
                heads = ps_o[:, 0:H * VW].rearrange("p (h w) -> p h w", w=VW)
                dve.wait_ge(o_ps, n + 1)
                if not early:
                    dve.wait_ge(attn_ready, n - 1)
                nc.vector.reciprocal(rsum[j % 2][:, :].unsqueeze(2), heads[:, :, HD:VW]).then_inc(rsum_ready, 1)
                dve.wait_ge(rsum_ready, n + 1)
                if j == 0 and not early:
                    dve.wait_ge(attnT_ps, s.t - 1 + FREE)
                nc.vector.tensor_tensor(attn[s.parity][:, j, :].rearrange("p (h d) -> p h d", d=HD),
                                        heads[:, :, 0:HD], rsum[j % 2][:, :].unsqueeze(2).to_broadcast([P, H, HD]),
                                        ALU.mult).then_inc(attn_ready, 1)

            def gate(s, r, bias, bank, ps_done, count, zT_read, done):
                dve.wait_ge(ps_done, count)
                dve.wait_ge(zT_read, s.t + FREE)
                nc.vector.scalar_tensor_tensor(per_batch(zT[:, :]), per_batch(bank[:, :]), biasT[:, bias:bias + 1],
                                               ada(r, s.t), ALU.add, ALU.mult).then_inc(done, 1)

            def gate1(s):
                gate(s, GATE1, O_B, ps_b, wo_ps, s.t + 1 + FREE, zT_ps, z_ready)

            def gate2(s):
                gate(s, GATE2, F2_B, ps_w[s.parity], w2_ps, s.t * FC + FC, z2T_ps, z2_ready)

            def low_of_hid(s, c):
                dve.wait_ge(hid_ready, s.t * FC + c + 1)
                nc.vector.tensor_tensor(hid_lo[:, c, :], hid[:, c, :], hid_hi[:, c, :],
                                        ALU.subtract).then_inc(hid_lo_ready, 1)

            def add_branch(s, ps_done, done):
                dve.wait_ge(ps_done, s.t + 1 + FREE)
                nc.vector.tensor_tensor(tokens(s.t), ps_b[:, :], tokens(s.t), ALU.add).then_inc(done, 1)

            for done in (x2_ready, z_ready, z2_ready, y_ready):
                dve.sem_inc(done, FREE)
            def stats_of(t):
                for j in range(SB):
                    group_stats(t, j)

            dve.memset(kexp[0][:, 0:ZERO_DVE, :], 0.0).then_inc(kexp_zero[0], 1)
            dve.wait_ge(x_in[0], 16)
            stats_of(0)
            dve.wait_ge(bn_done, SB)
            combine(0, SB, 0)
            dve.wait_ge(id_ready, 1)
            nc.vector.tensor_reduce(kmask[:, :], ident[:, :].rearrange("p (g h d) -> p h g d", g=HQ, h=Q4),
                                    axis=AX.XY, op=ALU.add).then_inc(kmask_ready, 1)
            dve.wait_ge(setupT_ready, 1)
            nc.vector.tensor_copy(condT[:, :], ps_b[:, 0:P]).then_inc(setupT_copied, 1)
            dve.wait_ge(rstd_ready, 1)
            for g in range(SB):
                c = slice(g * D, (g + 1) * D)
                last = nc.vector.tensor_scalar(xn[0][:, c], x_sb[:, c], mean[:, g:g + 1], rstd[:, g:g + 1],
                                               ALU.subtract, ALU.mult)
            last.then_inc(xn0_ready, 1)
            dve.wait_ge(setupT_ready, 2)
            nc.vector.tensor_copy(biasT[:, 0:NB0], ps_p[:, 0:NB0]).then_inc(setupT_copied, 1)
            dve.wait_ge(setupT_copied, 2)
            dve.wait_ge(kmask_ready, 1)
            nc.vector.tensor_scalar(kbias[:, :], kmask[:, :], biasT[:, K_B:K_B + 1], None, ALU.mult).then_inc(
                kbias_ready, 1)

            def take_condition(count, r, bank):
                dve.wait_ge(ada_ps, count)
                nc.vector.tensor_scalar(adaT[:, r, :], bank[:, :B], biasT[:, ADA_B + r:ADA_B + r + 1],
                                        1.0 if r in (SCALE1, SCALE2) else 0.0, ALU.add, ALU.add).then_inc(ada_ready, 1)

            take_condition(1, SCALE1, ps_o)
            take_condition(2, SHIFT1, ps_q)
            dve.wait_ge(ada_ready, 2)
            scale_h(Step(0, 0), 0, True)
            h0 = per_batch(hT[0][:, :])
            dve.wait_ge(h_scaled, 1)
            nc.vector.tensor_tensor(h0, h0, ada(SHIFT1, 0), ALU.add).then_inc(h0_ready, 1)
            dve.wait_ge(x_in[1], 16)
            stats_of(1)
            dve.wait_ge(bn_done, 2 * SB)
            combine(SB, 2 * SB, 1)

            def place_k0(piece, g):
                rows, c = slice(g * P // HQ, (g + 1) * P // HQ), K0_PIECES[piece]
                shape = [P // HQ, Q4, c.stop - c.start]
                return nc.vector.scalar_tensor_tensor(
                    kexp[0][rows, g * Q4:(g + 1) * Q4, c], ps_k[rows, c].unsqueeze(1).to_broadcast(shape),
                    biasT[rows, K_B:K_B + 1], kmask[rows, :].unsqueeze(2).to_broadcast(shape), ALU.add, ALU.mult)

            dve.wait_ge(kexp_zero[0], 3)
            dve.wait_ge(k_ps, 1)
            place_k0(0, 0)
            place_k0(0, 1).then_inc(k0_dve, 1)
            take_condition(3, GATE1, ps_s[0])
            take_condition(4, SHIFT2, ps_s[1])
            take_condition(5, SCALE2, ps_p)
            take_condition(6, GATE2, ps_b)
            nc.vector.tensor_reduce(vmask[:, :], ident[:, :].rearrange("p (h k) -> p h k", k=N),
                                    axis=AX.X, op=ALU.add).then_inc(vmask_ready, 1)
            dve.wait_ge(vmask_ready, 1)
            for p in range(2):
                nc.vector.tensor_copy(vexp[p][:, :, :, :, HD], vmask[:, :].unsqueeze(1).unsqueeze(3).to_broadcast(
                    [P, BS, Q4, HQ])).then_inc(vexp_ones, 1)
            place_k0(1, 0)
            scale_h(Step(0, 1), 0, True)
            place_k0(1, 1).then_inc(k0_dve, 1)
            dve.wait_ge(setupT_ready, 3)
            nc.vector.tensor_copy(biasT[:, NB0:NB0 + NB1], ps_p[:, 0:NB1]).then_inc(setupT_copied, 1)

            def attend(s, before, after):
                for j in range(SB):
                    n = s.t * SB + j
                    if j == 0 and before > 1:
                        gate1(s.plus(-2))
                    if j == 1 and before > 1:
                        add_branch(s.plus(-2), zT_ps, x2_ready)
                    if j == 2 and front_slot(before, after) == 1:
                        scale_h(*ahead(s, after))
                    if j == 3 and not before:
                        scale_h(*ahead(s, after))
                    if j == 2 and before > 1:
                        dve.wait_ge(x2_ready, s.t - 1 + FREE)
                    less_max(n, j, not before and j < 2)
                    if not before and j == 0:
                        v_blocks(s, True)
                    if j == 0 and before:
                        v_blocks(s)
                    if before == 1 and j == 0:
                        dve.wait_ge(whi_ready, 5)
                        for lo, whole, hi in ((w1_lo, w1_sb, w1_hi), (w2_lo, w2_sb, w2_hi)):
                            nc.vector.tensor_tensor(lo[:, :], whole[:, :], hi[:, :], ALU.subtract).then_inc(ff_wlo_ready, 1)
                    if before or j > 1:
                        normalize_heads(s if j > 1 else s.plus(-1), (j - 2) % SB, n - 2, not before)
                    if not before:
                        for t in ((2,), (3, 4), (5, 6), (7,))[j]:
                            dve.wait_ge(x_in[t], 16)
                            stats_of(t)
                            if t == 3:
                                dve.wait_ge(bn_done, 4 * SB)
                                combine(2 * SB, 4 * SB, 2)
                            if t == NS - 1:
                                dve.wait_ge(bn_done, GROUPS)
                                combine(4 * SB, GROUPS, 3)
                    if j == (2 if after else 3) and before > 1:
                        stats_of(s.t - 2)
                    if j == 3 and after == 1:
                        scale_h(*ahead(s, after))
                    if j == 0 and after == 1:
                        dve.wait_ge(xn_ready, NS)
                        dve.wait_ge(bn_done, GROUPS + 2 * SB)
                        combine(0, 2 * SB, 4)
                    if j == 1 and not after:
                        dve.wait_ge(bn_done, GROUPS + 5 * SB)
                        combine(2 * SB, 5 * SB, 5)

            superblocks(dve, attend)
            last_s = Step(NS // 2 - 1, 1)
            gate1(last_s.plus(-1))
            normalize_heads(last_s, SB - 2, GROUPS - 2, False)
            scale_h(Step(0, 1), 1)
            add_branch(last_s.plus(-1), zT_ps, x2_ready)
            normalize_heads(last_s, SB - 1, GROUPS - 1, False)
            low_of_hid(Step(0, 0), 0)
            low_of_hid(Step(0, 0), 1)
            dve.wait_ge(x2_ready, NS - 1 + FREE)
            stats_of(NS - 2)
            gate1(last_s)
            low_of_hid(Step(0, 0), 2)
            add_branch(last_s, zT_ps, x2_ready)
            low_of_hid(Step(0, 0), 3)
            scale_h(Step(1, 0), 1)
            def feed(s, before, after):
                if before:
                    low_of_hid(s, 0)
                    gate2(s.plus(-1))
                    low_of_hid(s, 1)
                    if before == 1:
                        dve.wait_ge(x2_ready, NS + FREE)
                        stats_of(NS - 1)
                        dve.wait_ge(bn_done, 2 * GROUPS)
                        combine(5 * SB, GROUPS, 6)
                    low_of_hid(s, 2)
                    add_branch(s.plus(-1), z2T_ps, y_ready)
                    low_of_hid(s, 3)
                if before and after > 1:
                    scale_h(s.plus(2), 1)

            superblocks(dve, feed)
            gate2(last_s)
            add_branch(last_s, z2T_ps, y_ready)


_INS = ['x', 'cond_1024', 'L0_cond_W_ada', 'L0_cond_b_ada', 'L0_cond_Wq', 'L0_cond_bq', 'L0_cond_Wk', 'L0_cond_bk',
        'L0_cond_Wv', 'L0_cond_bv', 'L0_cond_Wo', 'L0_cond_bo', 'L0_cond_W1', 'L0_cond_b1', 'L0_cond_W2',
        'L0_cond_b2']


def kernel(**inputs):
    import numpy as _np
    import concourse.bacc as _bacc
    from concourse import mybir as _mybir
    from concourse.bass_utils import run_bass_kernel_spmd as _run

    nc = _bacc.Bacc("TRN2", target_bir_lowering=False, num_devices=1)
    arrays, args = {}, []
    for name in _INS:
        a = _np.ascontiguousarray(inputs[name])
        arrays[f"in_{name}_dram"] = a
        args.append(nc.dram_tensor(f"in_{name}_dram", a.shape, _mybir.dt.from_np(a.dtype), kind="ExternalInput").ap())
    shape = inputs["x"].shape
    args.append(nc.dram_tensor("out_0_dram", shape, _mybir.dt.float32, kind="ExternalOutput").ap())
    dit_block(nc, *args)
    r = _run(nc, [arrays], core_ids=[0])
    return r.results[0]["out_0_dram"]
```
